# Optimizing a Trainium2 kernel written in Bass

```python
import numpy as np
import jax
import jax.numpy as jnp

def _softmax(x, axis=-1):
    return jax.nn.softmax(x, axis=axis)

def _gelu(x):
    return jax.nn.gelu(x, approximate=True)

def _silu(x):
    return jax.nn.silu(x)

def _sigmoid(x):
    return jax.nn.sigmoid(x)

def _layernorm(x, axis=-1, eps=1e-05):
    m = jnp.mean(x, axis=axis, keepdims=True)
    v = jnp.var(x, axis=axis, keepdims=True)
    return (x - m) / jnp.sqrt(v + eps)

def _scatter_add(tgt, idx, src, axis=0):
    return tgt.at[idx].add(src)

def _segment_sum(src, seg, n):
    return jax.ops.segment_sum(src, seg, n)
kernel_name = 'mk_macaron_d1_jaxref_r8_a52be8'

def setup_inputs(seed: int=0):
    np.random.seed(seed)
    _w = jnp.asarray

    def _L0_attn_setup():
        import jax, jax.numpy as jnp
        import numpy as np
        E = 256
        H = 3
        key = jax.random.key(seed)
        ks = jax.random.split(key, 6)
        B, N = (4, 256)
        x = jax.random.normal(ks[0], (B, N, E), dtype=jnp.float32)
        Wq = jax.random.normal(ks[1], (H, E, E), dtype=jnp.float32) * 0.02
        Wk = jax.random.normal(ks[2], (H, E, E), dtype=jnp.float32) * 0.02
        Wv = jax.random.normal(ks[3], (H, E, E), dtype=jnp.float32) * 0.02
        fc_w = jax.random.normal(ks[4], (E, E), dtype=jnp.float32) * 0.02
        fc_b = jax.random.normal(ks[5], (E,), dtype=jnp.float32) * 0.02
        return {'x': x, 'Wq': Wq, 'Wk': Wk, 'Wv': Wv, 'fc_w': fc_w, 'fc_b': fc_b}
    _L0_attn_in = _L0_attn_setup()

    def _L0_ffn_setup():
        import jax, jax.numpy as jnp
        import numpy as np
        B, S, H = (1, 128, 256)
        F = 128
        E = 16
        K = 2
        NS = 1
        ROUTE_SCALE = 1.0
        key = jax.random.key(seed)
        ks = jax.random.split(key, 8)

        def w(k, shape, fan_in):
            return jax.random.normal(k, shape, jnp.float32) * fan_in ** (-0.5)
        return {'hidden_states': jax.random.normal(ks[0], (B, S, H), jnp.float32), 'gate_w': w(ks[1], (H, E), H), 'expert_bias': jnp.zeros((E,), jnp.float32), 'shared_gate_w': w(ks[2], (H, F * NS), H), 'shared_up_w': w(ks[3], (H, F * NS), H), 'shared_down_w': w(ks[4], (F * NS, H), F * NS), 'experts_gate_up': w(ks[5], (E, H, 2 * F), H), 'experts_down': w(ks[6], (E, F, H), F)}
    _L0_ffn_in = _L0_ffn_setup()
    _d = {'L0_attn_x': _L0_attn_in['x'], 'L0_attn_Wq': _L0_attn_in['Wq'], 'L0_attn_Wk': _L0_attn_in['Wk'], 'L0_attn_Wv': _L0_attn_in['Wv'], 'L0_attn_fc_w': _L0_attn_in['fc_w'], 'L0_attn_fc_b': _L0_attn_in['fc_b'], 'L0_ffn_gate_w': _L0_ffn_in['gate_w'], 'L0_ffn_expert_bias': _L0_ffn_in['expert_bias'], 'L0_ffn_shared_gate_w': _L0_ffn_in['shared_gate_w'], 'L0_ffn_shared_up_w': _L0_ffn_in['shared_up_w'], 'L0_ffn_shared_down_w': _L0_ffn_in['shared_down_w'], 'L0_ffn_experts_gate_up': _L0_ffn_in['experts_gate_up'], 'L0_ffn_experts_down': _L0_ffn_in['experts_down']}
    _x0 = _d['L0_attn_x']
    _d['L0_attn_x'] = jax.random.normal(jax.random.fold_in(jax.random.key(seed), 1), (4, 512, 256), dtype=_x0.dtype)
    del _x0
    return _d

def reference(L0_attn_x, L0_attn_Wq, L0_attn_Wk, L0_attn_Wv, L0_attn_fc_w, L0_attn_fc_b, L0_ffn_gate_w, L0_ffn_expert_bias, L0_ffn_shared_gate_w, L0_ffn_shared_up_w, L0_ffn_shared_down_w, L0_ffn_experts_gate_up, L0_ffn_experts_down):

    def _L0_attn_ref(x, Wq, Wk, Wv, fc_w, fc_b):
        import jax, jax.numpy as jnp
        import numpy as np
        E = 256
        H = 3
        Q = jnp.einsum('bne,hde->hbnd', x, Wq)
        K = jnp.einsum('bne,hde->hbnd', x, Wk)
        V = jnp.einsum('bne,hde->hbnd', x, Wv)
        scale = 1.0 / jnp.sqrt(jnp.float32(E))
        scores = jnp.einsum('hbnd,hbmd->hbnm', Q, K) * scale
        w = jax.nn.softmax(scores, axis=2)
        attn = jnp.einsum('hbnm,hbmd->hbnd', w, V)
        mean = jnp.mean(attn, axis=0)
        return mean @ fc_w.T + fc_b

    def _L0_ffn_ref(hidden_states, gate_w, expert_bias, shared_gate_w, shared_up_w, shared_down_w, experts_gate_up, experts_down):
        import jax, jax.numpy as jnp
        import numpy as np
        B, S, H = (1, 128, 256)
        F = 128
        E = 16
        K = 2
        NS = 1
        ROUTE_SCALE = 1.0
        b, s, h = hidden_states.shape
        x = hidden_states.reshape(-1, h)
        T = x.shape[0]
        router_logits = (x @ gate_w).astype(jnp.float32)
        scores = jax.nn.sigmoid(router_logits)
        _, selected = jax.lax.top_k(scores + expert_bias[None, :], K)
        top_scores = jnp.take_along_axis(scores, selected, axis=1)
        top_scores = top_scores / (top_scores.sum(-1, keepdims=True) + 1e-20)
        top_scores = top_scores * ROUTE_SCALE
        shared = jax.nn.silu(x @ shared_gate_w) * (x @ shared_up_w) @ shared_down_w
        comb = jnp.zeros((T, E), jnp.float32).at[jnp.arange(T)[:, None], selected].add(top_scores)
        routed = jnp.zeros_like(x)
        for e in range(E):
            gu = x @ experts_gate_up[e]
            g, u = jnp.split(gu, 2, axis=-1)
            routed = routed + comb[:, e:e + 1] * (jax.nn.silu(g) * u @ experts_down[e])
        return (shared + routed).reshape(b, s, h)
    x = L0_attn_x
    x = x + 0.5 * _L0_ffn_ref(_layernorm(x, axis=-1), L0_ffn_gate_w, L0_ffn_expert_bias, L0_ffn_shared_gate_w, L0_ffn_shared_up_w, L0_ffn_shared_down_w, L0_ffn_experts_gate_up, L0_ffn_experts_down)
    x = x + _L0_attn_ref(_layernorm(x, axis=-1), L0_attn_Wq, L0_attn_Wk, L0_attn_Wv, L0_attn_fc_w, L0_attn_fc_b)
    x = x + 0.5 * _L0_ffn_ref(_layernorm(x, axis=-1), L0_ffn_gate_w, L0_ffn_expert_bias, L0_ffn_shared_gate_w, L0_ffn_shared_up_w, L0_ffn_shared_down_w, L0_ffn_experts_gate_up, L0_ffn_experts_down)
    return x

_drawn_inputs = setup_inputs


def setup_inputs(seed=0):
    import zlib

    import numpy as np

    out = dict(_drawn_inputs(seed))
    spreads = {'L0_ffn_expert_bias': (0.0, 0.1)}
    factors = {'L0_attn_Wq': 8.0,
     'L0_attn_Wk': 8.0,
     'L0_attn_Wv': 6.719,
     'L0_attn_fc_w': 7.094,
     'L0_attn_fc_b': 4.942}
    for name, (base, spread) in spreads.items():
        noise = np.random.default_rng([zlib.crc32(name.encode()), seed]).standard_normal(out[name].shape)
        drawn = base * np.exp(spread * noise) if base else spread * noise
        out[name] = jnp.asarray(drawn.astype(out[name].dtype))
    for name, factor in factors.items():
        out[name] = (out[name] * factor).astype(out[name].dtype)
    return out
```

```python
from contextlib import ExitStack

import numpy as np

import concourse.bass as bass
from concourse import mybir

F32 = mybir.dt.float32
F32R = mybir.dt.float32r
F16 = mybir.dt.float16
I32 = mybir.dt.int32
U32 = mybir.dt.uint32
ALU = mybir.AluOpType
ACT = mybir.ActivationFunctionType
AX = mybir.AxisListType.X

P = 128
BANK = 512


class Counter:

    def __init__(self, ctx, nc, name):
        self.handle = ctx.enter_context(nc.semaphore(name))
        self.value = 0

    def mark(self, instruction, by=1):
        instruction.then_inc(self.handle, by)
        self.value += by
        return (self, self.value)


def macaron(nc, x_in, w_pack, wq, wk, wv, fc_t, fc_b, gate, bias, out):
    B, N, H = x_in.shape
    T = B * N
    NT = T // P
    TB = N // P
    KH = H // P
    NW = w_pack.shape[0]
    E = NW - 1
    F = P
    HEADS = wq.shape[0]
    TOPK = 2
    SLOT_TILES = T * TOPK // P + E - 1
    EPS = 1e-5
    WCOLS = KH * 2 * F + H
    GU = 2 * F
    Q_SCALE = 1.0 / float(np.sqrt(H))

    x_rows = x_in.rearrange("b (t p) h -> (b t) p h", p=P)
    out_rows = out.rearrange("b (t p) h -> (b t) p h", p=P)
    xn_dram = nc.dram_tensor("xn_dram", (T, H), F32, kind="Internal").ap()
    y_dram = nc.dram_tensor("y_dram", (SLOT_TILES * P, H), F32, kind="Internal").ap()

    pe, act, dve, pool, sp = nc.tensor, nc.scalar, nc.vector, nc.gpsimd, nc.sync

    with ExitStack() as ctx:
        def sbuf(name, shape, dt):
            return ctx.enter_context(nc.sbuf_tensor(name, shape, dt))

        def counter(name):
            return Counter(ctx, nc, name)

        waited = {}

        def wait(engine, *tokens):
            for token in tokens:
                if token is None:
                    continue
                sem, value = token
                key = (id(engine), id(sem))
                if waited.get(key, 0) < value:
                    engine.wait_ge(sem.handle, value)
                    waited[key] = value

        x_sb = sbuf("x_sb", [P, NT, H], F32)
        w_hi = sbuf("w_hi", [P, NW * WCOLS], F32R)
        w_lo = sbuf("w_lo", [P, NW * WCOLS], F32R)
        a_sp = sbuf("a_sp", [P, 2, HEADS, KH, H], F32R)
        b_sp = sbuf("b_sp", [P, 2, HEADS, KH, H], F32R)
        xT = sbuf("xT", [P, 2, 2, KH, N], F32R)
        g_sp = sbuf("g_sp", [P, 2, KH, N], F32R)
        e_sp = sbuf("e_sp", [P, 2, 2, N], F32R)
        v_sp = sbuf("v_sp", [P, 2, 2, H], F32R)
        stage = sbuf("stage", [P, 2, WCOLS], F32)
        raw = sbuf("raw", [P, 2048], F32)
        route = sbuf("route", [P, 7, NT * E], F32)
        xn = sbuf("xn", [P, 2, H], F32)
        choice = sbuf("choice", [P, NT, E], F16)
        ident = sbuf("ident", [P, P], F32)
        before = sbuf("before", [P, P], F16)
        ones = sbuf("ones", [P, P], F16)
        fcb_sb = route[:, 6, 0:H]
        bias_sb = sbuf("bias_sb", [P, E], F32)
        gate_raw = sbuf("gate_raw", [P, KH, E], F32)
        gate_sp = sbuf("gate_sp", [P, 2, KH, E], F32R)
        expert_no = sbuf("expert_no", [P, E], F32)
        lane_no = sbuf("lane_no", [P, P], F16)
        tile_no = sbuf("tile_no", [P, SLOT_TILES + 1], F32)
        tile_no16 = sbuf("tile_no16", [P, SLOT_TILES + 1], F16)
        token_no = sbuf("token_no", [P, NT], F32)
        pick_lane = sbuf("pick_lane", [P, 2, P], F16)
        pick_tile = sbuf("pick_tile", [P, 2, SLOT_TILES + 1], F16)
        stats = sbuf("stats", [P, 2, 6], F32)
        moments = sbuf("moments", [P, 2, 2], F32)
        rstd = sbuf("rstd", [P, 2, 1], F32)
        minus_half = sbuf("minus_half", [P, 1], F32)
        top8 = sbuf("top8", [P, NT, 8], F32)
        top8_at = sbuf("top8_at", [P, NT, 8], U32)
        top_at = sbuf("top_at", [P, TOPK, NT], F32)
        weight = sbuf("weight", [P, TOPK, NT], F32)
        total_w = sbuf("total_w", [P, NT], F32)
        slot = sbuf("slot", [P, TOPK, NT], F32)
        slot_i = sbuf("slot_i", [P, TOPK, NT], I32)
        lane_i = sbuf("lane_i", [P, TOPK, NT], I32)
        slot_lane = sbuf("slot_lane", [P, TOPK, NT], F32)
        slot_tile = sbuf("slot_tile", [P, TOPK, NT], F32)
        count_i = sbuf("count_i", [P, 2, E], I32)
        ends = sbuf("ends", [P, 5, E], F32)
        tile_expert = sbuf("tile_expert", [1, SLOT_TILES + 1], F32)
        tile_expert_i = sbuf("tile_expert_i", [1, SLOT_TILES + 1], I32)
        gather_at = sbuf("gather_at", [P, SLOT_TILES + 1], U32)
        row_max = sbuf("row_max", [P, 2, 1], F32)
        row_sum = sbuf("row_sum", [P, 2, 1], F32)
        row_inv = sbuf("row_inv", [P, 2, 1], F32)
        bank = [ctx.enter_context(nc.psum_tensor(f"bank{i}", [P, BANK], F32)) for i in range(8)]

        s_const = counter("s_const")
        s_small = counter("s_small")
        s_fcb = counter("s_fcb")
        s_x = [counter(f"s_x{b}") for b in range(B)]
        s_stage = [counter(f"s_stage{i}") for i in range(2)]
        s_wsplit_hi = counter("s_wsplit_hi")
        s_wsplit_lo = counter("s_wsplit_lo")
        s_raw = [counter(f"s_raw{i}") for i in range(2)]
        s_fold = counter("s_fold")
        s_fold_hi = counter("s_fold_hi")
        s_fold_lo = counter("s_fold_lo")
        s_ln = counter("s_ln")
        s_rstd = counter("s_rstd")
        s_xn_out = [counter(f"s_xn_out{i}") for i in range(2)]
        s_t = counter("s_t")
        s_t_hi = counter("s_t_hi")
        s_t_lo = counter("s_t_lo")
        s_router = counter("s_router")
        s_score = counter("s_score")
        s_route = counter("s_route")
        s_rank = counter("s_rank")
        s_pick = counter("s_pick")
        s_inv = counter("s_inv")
        s_row = [counter(f"s_row{i}") for i in range(4)]
        s_xrow = [counter(f"s_xrow{i}") for i in range(4)]
        s_gu = counter("s_gu")
        s_silu = counter("s_silu")
        s_act = counter("s_act")
        s_hT = counter("s_hT")
        s_hT_hi = counter("s_hT_hi")
        s_hT_lo = counter("s_hT_lo")
        s_y = counter("s_y")
        s_y_act = counter("s_y_act")
        s_y_out = [counter(f"s_y_out{i}") for i in range(3)]
        s_pair = [counter(f"s_pair{i}") for i in range(6)]
        s_res = counter("s_res")
        s_g = counter("s_g")
        s_g_hi = counter("s_g_hi")
        s_g_lo = counter("s_g_lo")
        s_s = counter("s_s")
        s_max = counter("s_max")
        s_exp = counter("s_exp")
        s_e_hi = counter("s_e_hi")
        s_e_lo = counter("s_e_lo")
        s_v = counter("s_v")
        s_inv_sum = counter("s_inv_sum")
        s_v_hi = counter("s_v_hi")
        s_v_lo = counter("s_v_lo")
        s_o = counter("s_o")
        s_out = counter("s_out")

        def three_pass(dst, lhs, rhs, first=True, last=True):
            n = len(lhs)
            for k in range(n):
                for i, (l, r) in enumerate(((0, 0), (0, 1), (1, 0))):
                    m = pe.matmul(dst, lhs[k][l], rhs[k][r], start=(first and k == 0 and i == 0),
                                  stop=(last and k == n - 1 and i == 2), skip_group_check=True)
            return m

        pool.memset(ident[:], 0.0)
        pool.memset(before[:], 1.0)
        pool.memset(minus_half[:], -0.5)
        pool.iota(expert_no[:], [[1, E]], base=0, channel_multiplier=0, allow_small_or_imprecise_dtypes=True)
        pool.iota(lane_no[:], [[1, P]], base=0, channel_multiplier=0, allow_small_or_imprecise_dtypes=True)
        pool.iota(tile_no[:], [[P, SLOT_TILES + 1]], base=0, channel_multiplier=0,
                  allow_small_or_imprecise_dtypes=True)
        pool.iota(tile_no16[:], [[1, SLOT_TILES + 1]], base=0, channel_multiplier=0,
                  allow_small_or_imprecise_dtypes=True)
        pool.iota(token_no[:], [[P, NT]], base=0, channel_multiplier=1, allow_small_or_imprecise_dtypes=True)
        zeroed = s_const.mark(pool.memset(ones[:], 1.0))
        wait(pool, zeroed)
        pool.affine_select(out=ident[:], in_=ident[:], compare_op=ALU.not_equal, fill=1.0, base=0,
                           pattern=[[-1, P]], channel_multiplier=1)
        constants = s_const.mark(pool.affine_select(out=before[:], in_=before[:], compare_op=ALU.is_gt, fill=0.0,
                                                    base=0, pattern=[[1, P]], channel_multiplier=-1))

        x_loaded = []
        for b in range(B):
            x_loaded.append(s_x[b].mark(sp.dma_start(
                x_sb[:, b * TB:(b + 1) * TB, :], x_rows[b * TB:(b + 1) * TB].rearrange("t p h -> p t h")), 16))
            if b == 0:
                act.dma_start(gate_raw[:], gate.rearrange("(k p) e -> p k e", p=P)).then_inc(s_small.handle, 16)
                act.dma_start(bias_sb[:], bias).then_inc(s_small.handle, 16)
                s_small.value += 32
        small_loaded = (s_small, s_small.value)

        weight_ready = [None] * NW

        def split_weight(n, w):
            i = n % 2
            wait(sp, *split_done[i])
            loaded = s_stage[i].mark(sp.dma_start(stage[:, i, :], w_pack[w]), 16)
            cols = slice(w * WCOLS, (w + 1) * WCOLS)
            wait(act, loaded)
            hi = s_wsplit_hi.mark(act.copy(w_hi[:, cols], stage[:, i, :]))
            wait(pool, loaded, hi)
            lo = s_wsplit_lo.mark(pool.tensor_tensor(w_lo[:, cols], stage[:, i, :], w_hi[:, cols].bitcast(F32),
                                                     ALU.subtract))
            split_done[i] = [hi, lo]
            weight_ready[w] = [hi, lo]

        split_done = [[], []]

        raw_free = [[], []]

        def fold(n, head, is_v):
            i = n % 2
            half = raw[:, i * 1024:(i + 1) * 1024].rearrange("p (m k h) -> p m k h", m=2, k=KH)
            left, right = (wv[head], fc_t) if is_v else (wq[head], wk[head])
            wait(sp, *raw_free[i])
            sp.dma_start(half[:, 0], left.rearrange("(k p) h -> p k h", p=P)).then_inc(s_raw[i].handle, 16)
            s_raw[i].value += 16
            loaded = s_raw[i].mark(sp.dma_start(half[:, 1], right.rearrange("(k p) h -> p k h", p=P)), 16)
            dst, scale = (b_sp, 1.0 / HEADS) if is_v else (a_sp, Q_SCALE)
            wait(pe, loaded, *bank_free[i])
            for e in range(KH):
                for k in range(KH):
                    m = pe.matmul(bank[4 + i][:, e * H:(e + 1) * H], half[:, 0, k, e * P:(e + 1) * P], half[:, 1, k, :],
                                  start=(k == 0), stop=(k == KH - 1))
            made = s_fold.mark(m)
            raw_free[i] = [made]
            src = bank[4 + i][:, 0:KH * H].rearrange("p (k h) -> p k h", k=KH)
            wait(act, made)
            hi = s_fold_hi.mark(act.mul(dst[:, 0, head], src, scale))
            wait(dve, hi)
            lo = s_fold_lo.mark(dve.scalar_tensor_tensor(out=dst[:, 1, head], in0=src, scalar=scale,
                                                         in1=dst[:, 0, head].bitcast(F32),
                                                         op0=ALU.mult, op1=ALU.subtract))
            bank_free[i] = [lo]
            folded[(is_v, head)] = [hi, lo]

        bank_free = [[], []]
        folded = {}

        xn_count = [0]
        xn_free = [[], []]

        def layer_norm(t, x_ready):
            i = xn_count[0] % 2
            xn_count[0] += 1
            wait(dve, x_ready)
            st = s_ln.mark(dve.bn_stats(stats[:, i, :], x_sb[:, t, :]))
            wait(dve, st)
            mo = s_ln.mark(dve.bn_aggr(moments[:, i, :], stats[:, i, :]))
            wait(dve, mo)
            va = s_ln.mark(dve.tensor_scalar(moments[:, i, 1:2], moments[:, i, 1:2], EPS, None, ALU.add))
            wait(pool, va, constants)
            rs = s_rstd.mark(pool.tensor_tensor(rstd[:, i, :], moments[:, i, 1:2], minus_half[:], ALU.pow))
            wait(dve, rs, *xn_free[i])
            done = s_ln.mark(dve.tensor_scalar(xn[:, i, :], x_sb[:, t, :], moments[:, i, 0:1], rstd[:, i, :],
                                               ALU.subtract, ALU.mult))
            xn_free[i] = []
            return i, done

        def store_xn(t, i, ready):
            wait(sp, ready, *gathers_done)
            stored = s_xn_out[i].mark(sp.dma_start(xn_dram[t * P:(t + 1) * P, :], xn[:, i, :]), 16)
            xn_free[i].append(stored)
            return stored

        gathers_done = []
        t_free = [[], []]

        def transpose_split(src, src_ready, banks, hi_dst, lo_dst, dst_free):
            j = banks[0] % len(banks[1])
            banks[0] += 1
            number, free = banks[1][j]
            ps = bank[number][:, 0:KH * P].rearrange("p (k n) -> p k n", k=KH)
            wait(pe, constants, src_ready, *free)
            for k in range(KH):
                m = pe.transpose(ps[:, k, :], src[:, k * P:(k + 1) * P], ident[:])
            turned = s_t.mark(m)
            wait(act, turned, *dst_free)
            hi = s_t_hi.mark(act.copy(hi_dst, ps))
            wait(dve, hi, *dst_free)
            lo = s_t_lo.mark(dve.tensor_tensor(lo_dst, ps, hi_dst.bitcast(F32), ALU.subtract))
            banks[1][j] = (number, [hi, lo])
            return turned, hi, lo

        logits_bank = 6

        def router(t, xhl, ready, bank_ready=()):
            wait(pe, *ready, *gate_ready, *bank_ready)
            lhs = [[xhl[0][:, k, :], xhl[1][:, k, :]] for k in range(KH)]
            rhs = [[gate_sp[:, 0, k, :], gate_sp[:, 1, k, :]] for k in range(KH)]
            return s_router.mark(three_pass(bank[logits_bank][:, t * E:(t + 1) * E], lhs, rhs))

        wait(act, small_loaded)
        g_hi = s_fold_hi.mark(act.copy(gate_sp[:, 0], gate_raw[:]))
        wait(dve, g_hi, small_loaded)
        g_lo = s_fold_lo.mark(dve.tensor_tensor(gate_sp[:, 1], gate_raw[:], gate_sp[:, 0].bitcast(F32), ALU.subtract))
        gate_ready = [g_hi, g_lo]

        def flat(i):
            return route[:, i, :].rearrange("p (t e) -> p t e", t=NT)

        def routing(last_logits, before_choice=()):
            def step(instruction):
                tok = s_route.mark(instruction)
                wait(dve, tok)
                return tok

            score, biased, pick0, pick1, scan_a, work, where = [flat(i) for i in range(7)]
            scan_b = biased
            picks = [pick0, pick1]
            logits = bank[logits_bank][:, 0:NT * E].rearrange("p (t e) -> p t e", t=NT)
            wait(act, last_logits, *before_choice)
            scored = s_score.mark(act.activation(score, logits, ACT.Sigmoid))
            wait(dve, scored, small_loaded, constants)
            step(dve.tensor_tensor(biased, score, bias_sb[:].unsqueeze(1).to_broadcast([P, NT, E]), ALU.add))
            for t in range(NT):
                tok = s_route.mark(dve.max(top8[:, t, :], biased[:, t, :]))
            wait(dve, tok)
            for t in range(NT):
                tok = s_route.mark(dve.max_index(top8_at[:, t, :], top8[:, t, :], biased[:, t, :]))
            wait(dve, tok)
            step(dve.tensor_copy(top_at[:], top8_at[:, :, 0:TOPK].rearrange("p t k -> p k t")))
            for k in range(TOPK):
                tok = s_route.mark(dve.tensor_tensor(
                    picks[k], expert_no[:].unsqueeze(1).to_broadcast([P, NT, E]),
                    top_at[:, k, :].unsqueeze(2).to_broadcast([P, NT, E]), ALU.is_equal))
            wait(dve, tok)
            chosen = step(dve.tensor_tensor(choice[:], pick0, pick1, ALU.add))
            wait(pe, chosen, constants, *rank_bank_free)
            m = pe.matmul(bank[7][:, 0:NT * E], before[:], choice[:].rearrange("p t e -> p (t e)"),
                          start=True, stop=True)
            m = pe.matmul(bank[7][:, NT * E:2 * NT * E], ones[:], choice[:].rearrange("p t e -> p (t e)"),
                          start=True, stop=True)
            ranked = s_rank.mark(m)
            rank = bank[7][:, 0:NT * E].rearrange("p (t e) -> p t e", t=NT)
            total = bank[7][:, NT * E:2 * NT * E].rearrange("p (t e) -> p t e", t=NT)
            wait(dve, ranked)
            step(dve.tensor_copy(scan_a, total))
            a, c = scan_a, scan_b
            d = 1
            while d < NT:
                s_route.mark(dve.tensor_copy(c[:, 0:d, :], a[:, 0:d, :]))
                step(dve.tensor_tensor(c[:, d:NT, :], a[:, d:NT, :], a[:, 0:NT - d, :], ALU.add))
                a, c = c, a
                d *= 2
            step(dve.tensor_scalar(count_i[:, 0, :], a[:, NT - 1, :], float(P - 1), None, ALU.add))
            shift = P.bit_length() - 1
            step(dve.tensor_scalar(count_i[:, 1, :], count_i[:, 0, :], shift, shift,
                                   ALU.logical_shift_right, ALU.logical_shift_left))
            step(dve.tensor_copy(ends[:, 0, :], count_i[:, 1, :]))
            d, i = 1, 0
            while d < E:
                s_route.mark(dve.tensor_copy(ends[:, i + 1, 0:d], ends[:, i, 0:d]))
                step(dve.tensor_tensor(ends[:, i + 1, d:E], ends[:, i, d:E], ends[:, i, 0:E - d], ALU.add))
                d, i = d * 2, i + 1
            end = ends[:, i, :]
            step(dve.tensor_tensor(ends[:, 0, :], end, ends[:, 0, :], ALU.subtract))
            step(dve.tensor_tensor(c, a, total, ALU.subtract))
            step(dve.tensor_tensor(work, c, ends[:, 0, :].unsqueeze(1).to_broadcast([P, NT, E]), ALU.add))
            step(dve.tensor_tensor(where, rank, work, ALU.add))
            for k in range(TOPK):
                step(dve.tensor_tensor(work, picks[k], where, ALU.mult))
                step(dve.tensor_reduce(slot[:, k, :], work, AX, ALU.add))
            slots = step(dve.tensor_copy(slot_i[:], slot[:]))
            step(dve.tensor_scalar(lane_i[:], slot_i[:], P - 1, None, ALU.bitwise_and))
            step(dve.tensor_copy(slot_lane[:], lane_i[:]))
            step(dve.tensor_scalar(lane_i[:], slot_i[:], shift, None, ALU.logical_shift_right))
            step(dve.tensor_copy(slot_tile[:], lane_i[:]))
            index = bank[logits_bank][:, 0:SLOT_TILES + 1]
            used = [None, None]
            n = 0
            for t in range(NT):
                for k in range(TOPK):
                    i = n % 2
                    wait(dve, used[i])
                    s_pick.mark(dve.tensor_scalar(pick_lane[:, i, :], lane_no[:], slot_lane[:, k, t:t + 1], None,
                                                  ALU.is_equal))
                    made = s_pick.mark(dve.tensor_scalar(pick_tile[:, i, :], tile_no16[:], slot_tile[:, k, t:t + 1],
                                                         token_no[:, t:t + 1], ALU.is_equal, ALU.mult))
                    wait(pe, made, scored)
                    used[i] = s_inv.mark(pe.matmul(index, pick_lane[:, i, :], pick_tile[:, i, :],
                                                   start=(n == 0), stop=(n == NT * TOPK - 1)))
                    n += 1
            wait(dve, used[1])
            indexed = s_route.mark(dve.tensor_copy(gather_at[:], index))
            cmp = route[0:1, 4:7, :].rearrange("p a b -> p (a b)")[:, 0:SLOT_TILES * E].rearrange(
                "p (j e) -> p j e", e=E) if SLOT_TILES * E <= 3 * NT * E else None
            step(dve.tensor_tensor(cmp, ends[0:1, i_end(E), :].unsqueeze(1).to_broadcast([1, SLOT_TILES, E]),
                                   tile_no[0:1, 0:SLOT_TILES].unsqueeze(2).to_broadcast([1, SLOT_TILES, E]),
                                   ALU.is_le))
            step(dve.tensor_reduce(tile_expert[:, 0:SLOT_TILES], cmp, AX, ALU.add))
            experts = step(dve.tensor_scalar(tile_expert_i[:, 0:SLOT_TILES], tile_expert[:, 0:SLOT_TILES],
                                             float(E - 1), None, ALU.min))
            for k in range(TOPK):
                step(dve.tensor_tensor(work, picks[k], score, ALU.mult))
                step(dve.tensor_reduce(weight[:, k, :], work, AX, ALU.add))
            step(dve.tensor_tensor(total_w[:], weight[:, 0, :], weight[:, 1, :], ALU.add))
            step(dve.tensor_scalar(total_w[:], total_w[:], 1e-20, None, ALU.add))
            step(dve.reciprocal(total_w[:], total_w[:]))
            for k in range(TOPK):
                weights = step(dve.scalar_tensor_tensor(out=weight[:, k, :], in0=weight[:, k, :], scalar=0.5,
                                                        in1=total_w[:], op0=ALU.mult, op1=ALU.mult))
            return dict(indexed=indexed, slots=slots, experts=experts, weights=weights)

        def i_end(n):
            return (n - 1).bit_length()

        row_buf = raw[:, 0:1024].rearrange("p (i h) -> p i h", i=4)
        y_buf = raw[:, 1024:1792].rearrange("p (i h) -> p i h", i=3)
        h_buf = raw[:, 1792:2048].rearrange("p (i f) -> p i f", i=2)
        xt_rows = xT[:].rearrange("p a b k n -> p (a b k n)").rearrange("p (i s k n) -> p i s k n", s=2, k=KH, n=P)
        ht_rows = g_sp[:].rearrange("p a k n -> p (a k n)").rearrange("p (i s n) -> p i s n", s=2, n=P)

        def mlp(load_row, n_tiles, weights_of, sink, state):
            S = state
            for s in range(n_tiles + 3):
                if s < n_tiles:
                    i = s % 4
                    row_ready = load_row(s, i, S["row_free"][i])
                    x_i = s % 3
                    turned, hi, lo = transpose_split(row_buf[:, i, :], row_ready, S["t_banks"], xt_rows[:, x_i, 0],
                                                     xt_rows[:, x_i, 1], S["xt_free"][x_i])
                    S["row_free"][i] = [turned]
                    S["xt_ready"][x_i] = [hi, lo]
                d = s - 3
                if d >= 0:
                    wait(pe, S["h_ready"][d % 2], *S["hT_bank_free"])
                    turned = s_hT.mark(pe.transpose(bank[4][:, 0:P], h_buf[:, d % 2, :], ident[:]))
                    S["h_free"][d % 2] = [turned]
                    wait(act, turned, *S["ht_free"][d % 2])
                    hhi = s_hT_hi.mark(act.copy(ht_rows[:, d % 2, 0], bank[4][:, 0:P]))
                    wait(dve, hhi)
                    hlo = s_hT_lo.mark(dve.tensor_tensor(ht_rows[:, d % 2, 1], bank[4][:, 0:P],
                                                         ht_rows[:, d % 2, 0].bitcast(F32), ALU.subtract))
                    S["hT_bank_free"] = [hhi, hlo]
                g = s - 1
                if 0 <= g < n_tiles:
                    pair = weights_of(g)
                    x_i = g % 3
                    wait(pe, *S["xt_ready"][x_i], *S["gu_free"][g % 2])
                    gu = bank[2 + g % 2][:, 0:GU]
                    lhs = [[xt_rows[:, x_i, part, k, :] for part in range(2)] for k in range(KH)]
                    rhs = [[pair(part, k * GU, GU) for part in range(2)] for k in range(KH)]
                    done = s_gu.mark(three_pass(gu, lhs, rhs))
                    S["xt_free"][x_i] = [done]
                    S["pair"][g % 4] = pair
                    wait(act, done, *S["h_free"][g % 2])
                    sil = s_silu.mark(act.activation(h_buf[:, g % 2, :], gu[:, 0:F], ACT.Silu))
                    wait(dve, sil)
                    S["h_ready"][g % 2] = s_act.mark(dve.tensor_tensor(h_buf[:, g % 2, :], h_buf[:, g % 2, :],
                                                                       gu[:, F:GU], ALU.mult))
                    S["gu_free"][g % 2] = [S["h_ready"][g % 2]]
                if d >= 0:
                    pair = S["pair"][d % 4]
                    wait(pe, hhi, hlo, *S["y_free"])
                    y = bank[5][:, 0:H]
                    made = s_y.mark(three_pass(y, [[ht_rows[:, d % 2, 0], ht_rows[:, d % 2, 1]]],
                                               [[pair(0, KH * GU, H), pair(1, KH * GU, H)]]))
                    S["ht_free"][d % 2] = [made]
                    S["y_free"] = [sink(d, y, made)]

        def mlp_state(t_banks):
            return dict(row_free=[[] for _ in range(4)], xt_free=[list(xt_users) for _ in range(3)],
                        xt_ready=[None] * 3, h_ready=[None] * 2, h_free=[[], []], hT_bank_free=[], ht_free=[[], []],
                        gu_free=[[], []], y_free=[], pair=[None] * 4, t_banks=t_banks)

        xt_users = []

        y_stores = [[], [], []]
        store_tokens = {}

        def ffn_tiles(state, routed, xn_stored, residual_ready):
            def shared_rows(j, i, free):
                wait(sp, *xn_stored, *free)
                return s_xrow[i].mark(sp.dma_start(row_buf[:, i, :], xn_dram[j * P:(j + 1) * P, :]), 16)

            def shared_weights(j):
                wait(pe, *weight_ready[E])
                return lambda part, at, n: (w_hi, w_lo)[part][:, E * WCOLS + at:E * WCOLS + at + n]

            def shared_sink(j, y, made):
                wait(dve, made, residual_ready[j])
                residual_ready[j] = s_res.mark(dve.scalar_tensor_tensor(
                    out=x_sb[:, j, :], in0=y, scalar=0.5, in1=x_sb[:, j, :], op0=ALU.mult, op1=ALU.add))
                return residual_ready[j]

            mlp(shared_rows, NT, shared_weights, shared_sink, state)
            routed.update(route_now())

            last_gather = []

            def slot_rows(j, i, free):
                wait(pool, *xn_stored, routed["indexed"], *free)
                tok = s_row[i].mark(pool.indirect_dma_start(
                    row_buf[:, i, :], None, xn_dram, bass.IndirectOffsetOnAxis(ap=gather_at[:, j:j + 1], axis=0)), 16)
                store_tokens[("row", i)] = tok
                return tok

            def slot_weights(j):
                wait(pe, routed["experts"])
                if j == 0:
                    for w in range(NW):
                        wait(pe, *weight_ready[w])
                base = pe.value_load(tile_expert_i[0:1, j:j + 1], min_val=0, max_val=E - 1) * WCOLS
                return lambda part, at, n: (w_hi, w_lo)[part][:, bass.ds(base + at, n)]

            def slot_sink(j, y, made):
                i = j % 3
                wait(act, made, *y_stores[i])
                copied = s_y_act.mark(act.copy(y_buf[:, i, :], y))
                wait(sp, copied, *pairs_read)
                stored = s_y_out[i].mark(sp.dma_start(y_dram[j * P:(j + 1) * P, :], y_buf[:, i, :]), 16)
                y_stores[i] = [stored]
                return copied

            mlp(slot_rows, SLOT_TILES, slot_weights, slot_sink, state)
            gathers_done[:] = [store_tokens[("row", i)] for i in range(4)]

        pairs_read = []
        pair_buf = stage[:].rearrange("p a b -> p (a b)").rearrange("p (i h) -> p i h", i=6)
        pair_free = [[] for _ in range(6)]

        def gather_pair(t, routed):
            toks = []
            for k in range(TOPK):
                i = (t * TOPK + k) % 6
                wait(pool, routed["slots"], *[s for ss in y_stores for s in ss], *pair_free[i],
                     *split_done[0], *split_done[1])
                toks.append(s_pair[i].mark(pool.indirect_dma_start(
                    pair_buf[:, i, :], None, y_dram,
                    bass.IndirectOffsetOnAxis(ap=slot_i[:, k, t:t + 1].bitcast(U32), axis=0)), 16))
            pairs_read[:] = pairs_read[-5:] + toks if len(pairs_read) > 5 else pairs_read + toks
            return toks

        def combine(t, toks, routed, ready):
            for k in range(TOPK):
                i = (t * TOPK + k) % 6
                wait(dve, toks[k], ready, routed["weights"])
                ready = s_res.mark(dve.scalar_tensor_tensor(
                    out=x_sb[:, t, :], in0=pair_buf[:, i, :], scalar=weight[:, k, t:t + 1], in1=x_sb[:, t, :],
                    op0=ALU.mult, op1=ALU.add))
                pair_free[i] = [ready]
            return ready

        def front(t, x_ready, t_banks, buf, buf_free, bank_ready=()):
            i, done = layer_norm(t, x_ready)
            stored = store_xn(t, i, done)
            turned, hi, lo = transpose_split(xn[:, i, :], done, t_banks, buf[0], buf[1], buf_free)
            xn_free[i].append(turned)
            logit = router(t, buf, [hi, lo], bank_ready)
            return stored, logit

        t_banks = [0, [(0, []), (1, [])]]
        order = [E] + list(range(E))
        xt_free_now = [[] for _ in range(3)]
        stored, logit = [], None
        residual = [x_loaded[t // TB] for t in range(NT)]
        n_split = n_fold = 0
        for t in range(NT):
            buf = (xt_rows[:, t % 3, 0], xt_rows[:, t % 3, 1])
            st, logit = front(t, residual[t], t_banks, buf, xt_free_now[t % 3])
            xt_free_now[t % 3] = [logit]
            stored.append(st)
            if n_split < NW:
                split_weight(n_split, order[n_split])
                n_split += 1
        while n_split < NW:
            split_weight(n_split, order[n_split])
            n_split += 1
        for is_v in (False, True):
            for head in range(HEADS):
                if n_fold >= 6:
                    break
                fold(n_fold, head, is_v)
                n_fold += 1
        rank_bank_free = []
        xt_users[:] = [logit]
        state = mlp_state(t_banks)
        state["hT_bank_free"], state["y_free"] = bank_free
        for i in range(4):
            state["row_free"][i] = raw_free[0] + raw_free[1]

        def route_now():
            return routing(logit)

        routed1 = {}
        ffn_tiles(state, routed1, stored, residual)
        E_users = [routed1["weights"]]

        attn_in = [None] * NT
        wait(sp, routed1["weights"])
        fcb_loaded = s_fcb.mark(sp.dma_start(fcb_sb, fc_b), 16)

        def attn_front(t):
            b = t // TB
            toks = gather_pair(t, routed1)
            ready = combine(t, toks, routed1, residual[t])
            i, done = layer_norm(t, ready)
            cols = slice((t % TB) * P, (t % TB + 1) * P)
            turned, hi, lo = transpose_split(xn[:, i, :], done, attn_t_banks, xT[:, b % 2, 0, :, cols],
                                             xT[:, b % 2, 1, :, cols], xt_batch_free[b % 2])
            xn_free[i].append(turned)
            wait(dve, ready, done, fcb_loaded)
            residual[t] = s_res.mark(dve.tensor_tensor(x_sb[:, t, :], x_sb[:, t, :], fcb_sb, ALU.add))
            attn_in[t] = [hi, lo]

        last_mlp = [state["y_free"][0], *state["hT_bank_free"], *state["gu_free"][0], *state["gu_free"][1],
                    *state["ht_free"][0], *state["ht_free"][1], *t_banks[1][0][1], *t_banks[1][1][1],
                    *state["xt_free"][0], *state["xt_free"][1], *state["xt_free"][2]]
        attn_t_banks = [0, [(7, [routed1["weights"]])]]
        xt_batch_free = [list(last_mlp), list(last_mlp)]
        for t in range(TB):
            attn_front(t)
        e32 = route[:].rearrange("p a b -> p (a b)")[:, 0:2 * N].rearrange("p (i n) -> p i n", i=2)
        S_BANKS, G_BANK, V_BANK, O_BANKS = (0, 1), 2, 3, (4, 5)
        g_bank_free, g_free = list(last_mlp), list(last_mlp)
        s_free = [list(last_mlp), list(last_mlp)]
        v_bank_free = list(last_mlp)
        e_free, v_free, e32_free = [[], []], [[], []], [list(E_users), list(E_users)]
        o_free = list(last_mlp)
        g_ready = [None, None]
        units = [(b, h, m) for b in range(B) for h in range(HEADS) for m in range(TB)]
        scores_done, pv_ready = {}, {}

        def make_g(b, h, f):
            nonlocal g_bank_free
            wait(pe, *[tok for t in range(b * TB, (b + 1) * TB) for tok in attn_in[t]], *folded[(False, h)],
                 *g_bank_free)
            lhs = [[a_sp[:, part, h, k, f * P:(f + 1) * P] for part in range(2)] for k in range(KH)]
            rhs = [[xT[:, b % 2, part, k, :] for part in range(2)] for k in range(KH)]
            made = s_g.mark(three_pass(bank[G_BANK][:], lhs, rhs))
            wait(act, made, *g_free)
            hi = s_g_hi.mark(act.copy(g_sp[:, 0, f, :], bank[G_BANK][:]))
            wait(dve, hi)
            lo = s_g_lo.mark(dve.tensor_tensor(g_sp[:, 1, f, :], bank[G_BANK][:], g_sp[:, 0, f, :].bitcast(F32),
                                               ALU.subtract))
            g_bank_free = [hi, lo]
            g_ready[f] = [hi, lo]
            return made

        def attn_scores(u):
            b, h, m = units[u]
            i = u % 2
            keys = slice(m * P, (m + 1) * P)
            wait(pe, *g_ready[0], *g_ready[1], *s_free[i])
            lhs = [[xT[:, b % 2, part, k, keys] for part in range(2)] for k in range(KH)]
            rhs = [[g_sp[:, part, k, :] for part in range(2)] for k in range(KH)]
            s_ps = bank[S_BANKS[i]][:]
            done = s_s.mark(three_pass(s_ps, lhs, rhs))
            scores_done[u] = done
            wait(dve, done)
            mx = s_max.mark(dve.tensor_reduce(row_max[:, i, :], s_ps, AX, ALU.max, negate=True))
            wait(act, mx, *e32_free[i])
            ex = s_exp.mark(act.activation(e32[:, i, :], s_ps, ACT.Exp, bias=row_max[:, i, :],
                                           accum_out=row_sum[:, i, :]))
            s_free[i] = [ex]
            return ex

        def attn_split(u, ex):
            i = u % 2
            wait(pool, ex, *e_free[i])
            hi = s_e_hi.mark(pool.tensor_copy(e_sp[:, i, 0, :], e32[:, i, :]))
            wait(dve, ex)
            iv = s_inv_sum.mark(dve.reciprocal(row_inv[:, i, :], row_sum[:, i, :]))
            wait(dve, hi, *e_free[i])
            lo = s_e_lo.mark(dve.tensor_tensor(e_sp[:, i, 1, :], e32[:, i, :], e_sp[:, i, 0, :].bitcast(F32),
                                               ALU.subtract))
            e32_free[i] = [hi, lo]
            return iv, hi, lo

        def attn_values(u, iv, e_hi, e_lo):
            nonlocal v_bank_free
            b, h, m = units[u]
            i = u % 2
            keys = slice(m * P, (m + 1) * P)
            wait(pe, *v_bank_free, *folded[(True, h)])
            v_ps = bank[V_BANK][:, 0:H]
            lhs = [[xT[:, b % 2, part, k, keys] for part in range(2)] for k in range(KH)]
            rhs = [[b_sp[:, part, h, k, :] for part in range(2)] for k in range(KH)]
            made = s_v.mark(three_pass(v_ps, lhs, rhs))
            wait(act, made, iv, *v_free[i])
            hi = s_v_hi.mark(act.mul(v_sp[:, i, 0, :], v_ps, row_inv[:, i, :]))
            wait(dve, hi, *v_free[i])
            lo = s_v_lo.mark(dve.scalar_tensor_tensor(out=v_sp[:, i, 1, :], in0=v_ps, scalar=row_inv[:, i, :],
                                                      in1=v_sp[:, i, 0, :].bitcast(F32), op0=ALU.mult,
                                                      op1=ALU.subtract))
            v_bank_free = [hi, lo]
            pv_ready[u] = [e_hi, e_lo, hi, lo]
            return made

        def attn_mix(u):
            b, h, m = units[u]
            i = u % 2
            first, last = (h == 0 and m == 0), (h == HEADS - 1 and m == TB - 1)
            wait(pe, *pv_ready[u], *(o_free if first else []))
            for q in range(TB):
                dst = bank[O_BANKS[q // 2]][:, (q % 2) * H:(q % 2 + 1) * H]
                lhs = [[e_sp[:, i, part, q * P:(q + 1) * P] for part in range(2)]]
                rhs = [[v_sp[:, i, part, :] for part in range(2)]]
                mm = three_pass(dst, lhs, rhs, first=(first and q % 2 == 0), last=last)
            done = s_o.mark(mm)
            e_free[i], v_free[i] = [done], [done]
            return done

        def attn_out(b, done):
            nonlocal o_free
            for q in range(TB):
                t = b * TB + q
                wait(dve, done, residual[t])
                residual[t] = s_res.mark(dve.tensor_tensor(
                    x_sb[:, t, :], x_sb[:, t, :], bank[O_BANKS[q // 2]][:, (q % 2) * H:(q % 2 + 1) * H], ALU.add))
            o_free = [residual[t]]

        make_g(0, 0, 0)
        make_g(0, 0, 1)
        U = len(units)
        per_batch = HEADS * TB
        for u in range(U + 2):
            if u < U:
                b, h, m = units[u]
                ex = attn_scores(u)
                nxt = units[u + 1] if (m == TB - 1 and u + 1 < U) else None
                if nxt:
                    g_free = [scores_done[u]]
                    make_g(nxt[0], nxt[1], 0)
            if u >= 2:
                done = attn_mix(u - 2)
                if (u - 2) % per_batch == per_batch - 1:
                    attn_out((u - 2) // per_batch, done)
            if u < U:
                if nxt:
                    make_g(nxt[0], nxt[1], 1)
                iv, e_hi, e_lo = attn_split(u, ex)
                vmade = attn_values(u, iv, e_hi, e_lo)
                if u % per_batch == per_batch - 1:
                    xt_batch_free[b % 2] = [vmade, scores_done[u]]
                if b + 1 < B and u % per_batch in (1, 3, 5, 7):
                    attn_front((b + 1) * TB + (u % per_batch) // 2)

        attention_done = [done, *o_free, *xt_batch_free[0], *xt_batch_free[1], *s_free[0], *s_free[1], *v_bank_free,
                          *g_bank_free]
        t_banks = [0, [(0, list(attention_done)), (1, list(attention_done))]]
        xt_free_now = [list(attention_done) for _ in range(3)]
        stored = []
        for t in range(NT):
            buf = (xt_rows[:, t % 3, 0], xt_rows[:, t % 3, 1])
            st, logit = front(t, residual[t], t_banks, buf, xt_free_now[t % 3], [routed1["indexed"]])
            xt_free_now[t % 3] = [logit]
            stored.append(st)
        xt_users[:] = [logit, done]
        state = mlp_state(t_banks)
        state["gu_free"] = [list(attention_done), list(attention_done)]
        state["y_free"] = list(attention_done)
        state["hT_bank_free"] = list(attention_done)
        state["ht_free"] = [list(attention_done), list(attention_done)]
        rank_bank_free = [tok for _, free in attn_t_banks[1] for tok in free]

        def route_now():
            return routing(logit, [*e32_free[0], *e32_free[1]])

        routed2 = {}
        ffn_tiles(state, routed2, stored, residual)
        for t in range(NT):
            toks = gather_pair(t, routed2)
            ready = combine(t, toks, routed2, residual[t])
            wait(sp, ready)
            stored_out = s_out.mark(sp.dma_start(out_rows[t], x_sb[:, t, :]), 16)
        wait(sp, stored_out)


def kernel(L0_attn_x, L0_attn_Wq, L0_attn_Wk, L0_attn_Wv, L0_attn_fc_w, L0_attn_fc_b, L0_ffn_gate_w,
           L0_ffn_expert_bias, L0_ffn_shared_gate_w, L0_ffn_shared_up_w, L0_ffn_shared_down_w,
           L0_ffn_experts_gate_up, L0_ffn_experts_down):
    import concourse.bacc as bacc
    from concourse.bass_utils import run_bass_kernel_spmd

    shared_gu = np.concatenate([L0_ffn_shared_gate_w, L0_ffn_shared_up_w], axis=1)[None]
    gate_up = np.concatenate([L0_ffn_experts_gate_up, shared_gu])
    down = np.concatenate([L0_ffn_experts_down, np.asarray(L0_ffn_shared_down_w)[None]])
    nw, hidden, gu = gate_up.shape
    gate_up = gate_up.reshape(nw, hidden // P, P, gu).transpose(0, 2, 1, 3).reshape(nw, P, -1)
    arrays = {
        "x": L0_attn_x,
        "w_pack": np.concatenate([gate_up, down], axis=2),
        "wq": L0_attn_Wq,
        "wk": L0_attn_Wk,
        "wv": L0_attn_Wv,
        "fc_t": np.asarray(L0_attn_fc_w).T,
        "fc_b": np.broadcast_to(np.asarray(L0_attn_fc_b), (P, hidden)),
        "gate": L0_ffn_gate_w,
        "bias": np.broadcast_to(np.asarray(L0_ffn_expert_bias), (P, nw - 1)),
    }
    arrays = {f"in_{k}": np.ascontiguousarray(v) for k, v in arrays.items()}
    nc = bacc.Bacc("TRN2", target_bir_lowering=False, num_devices=1)
    args = [nc.dram_tensor(k, v.shape, mybir.dt.from_np(v.dtype), kind="ExternalInput").ap() for k, v in arrays.items()]
    out = nc.dram_tensor("out", arrays["in_x"].shape, F32, kind="ExternalOutput").ap()
    macaron(nc, *args, out)
    result = run_bass_kernel_spmd(nc, [arrays], core_ids=[0])
    return result.results[0]["out"]
```

```python
from contextlib import ExitStack

import numpy as np

import concourse.bass as bass
from concourse import mybir

F32 = mybir.dt.float32
F32R = mybir.dt.float32r
F16 = mybir.dt.float16
I32 = mybir.dt.int32
U32 = mybir.dt.uint32
ALU = mybir.AluOpType
ACT = mybir.ActivationFunctionType
AX = mybir.AxisListType.X

P = 128
BANK = 512


class Counter:

    def __init__(self, ctx, nc, name):
        self.handle = ctx.enter_context(nc.semaphore(name))
        self.value = 0

    def mark(self, instruction, by=1):
        instruction.then_inc(self.handle, by)
        self.value += by
        return (self, self.value)


def tiles_per_word(experts):
    return 24 // (experts.bit_length() - 1)


def macaron(nc, x_in, w_pack, wq, wk, wv, fc_t, fc_b, gate, bias, pack, out):
    B, N, H = x_in.shape
    T = B * N
    NT = T // P
    TB = N // P
    KH = H // P
    NW = w_pack.shape[0]
    E = NW - 1
    F = P
    HEADS = wq.shape[0]
    TOPK = 2
    PAIRS = 6
    PICKS = 4
    SLOT_TILES = T * TOPK // P + E - 1
    EPS = 1e-5
    WCOLS = KH * 2 * F + H
    GU = 2 * F
    XN_BUFS = 4
    E_BITS = E.bit_length() - 1
    WORDS = pack.shape[1]
    PER_LOAD = tiles_per_word(E)
    Q_SCALE = 1.0 / float(np.sqrt(H))

    x_rows = x_in.rearrange("b (t p) h -> (b t) p h", p=P)
    out_rows = out.rearrange("b (t p) h -> (b t) p h", p=P)
    xn_dram = nc.dram_tensor("xn_dram", (T, H), F32, kind="Internal").ap()
    y_dram = nc.dram_tensor("y_dram", (SLOT_TILES * P, H), F32, kind="Internal").ap()

    pe, act, dve, pool, sp = nc.tensor, nc.scalar, nc.vector, nc.gpsimd, nc.sync

    with ExitStack() as ctx:
        def sbuf(name, shape, dt):
            return ctx.enter_context(nc.sbuf_tensor(name, shape, dt))

        def counter(name):
            return Counter(ctx, nc, name)

        waited = {}

        def wait(engine, *tokens):
            for token in tokens:
                if token is None:
                    continue
                sem, value = token
                key = (id(engine), id(sem))
                if waited.get(key, 0) < value:
                    engine.wait_ge(sem.handle, value)
                    waited[key] = value

        x_sb = sbuf("x_sb", [P, NT, H], F32)
        w_hi = sbuf("w_hi", [P, NW * WCOLS], F32R)
        w_lo = sbuf("w_lo", [P, NW * WCOLS], F32R)
        a_sp = sbuf("a_sp", [P, 2, HEADS, KH, H], F32R)
        b_sp = sbuf("b_sp", [P, 2, HEADS, KH, H], F32R)
        xT = sbuf("xT", [P, 2, 2, KH, N], F32R)
        g_sp = sbuf("g_sp", [P, 2, KH, N], F32R)
        e_sp = sbuf("e_sp", [P, 2, 2, N], F32R)
        v_sp = sbuf("v_sp", [P, 2, 2, H], F32R)
        stage = sbuf("stage", [P, 2 * WCOLS], F32)
        raw = sbuf("raw", [P, 2048], F32)
        route = sbuf("route", [P, 7, NT * E], F32)
        xn = sbuf("xn", [P, 2, H], F32)
        choice = sbuf("choice", [P, NT, E], F16)
        ident = sbuf("ident", [P, P], F32)
        before = sbuf("before", [P, P], F16)
        ones = sbuf("ones", [P, P], F16)
        fcb_sb = route[:, 6, 0:H]
        bias_sb = sbuf("bias_sb", [P, E], F32)
        gate_raw = sbuf("gate_raw", [P, KH, E], F32)
        expert_no = sbuf("expert_no", [P, E], F32)
        lane_no = sbuf("lane_no", [P, P], F16)
        tile_no16 = sbuf("tile_no16", [P, SLOT_TILES + 1], F16)
        token_no = sbuf("token_no", [P, NT], F32)
        pick_lane = sbuf("pick_lane", [P, PICKS, P], F16)
        pick_tile = sbuf("pick_tile", [P, PICKS, SLOT_TILES + 1], F16)
        stats = sbuf("stats", [P, 3, TB, 6], F32)
        moments = sbuf("moments", [P, NT, 2], F32)
        variance = sbuf("variance", [P, NT], F32)
        rstd = sbuf("rstd", [P, NT], F32)
        columns = sbuf("columns", [P, TB + 2], F32)
        minus_half, tile_start, tile_expert = columns[:, 0:TB], columns[:, TB:TB + 1], columns[:, TB + 1:TB + 2]
        top8 = sbuf("top8", [P, NT, 8], F32)
        top8_at = sbuf("top8_at", [P, NT, 8], U32)
        top_at = sbuf("top_at", [P, TOPK, NT], F32)
        weight = sbuf("weight", [P, TOPK, NT], F32)
        total_w = sbuf("total_w", [P, NT], F32)
        slot = sbuf("slot", [P, TOPK, NT], F32)
        slot_i = sbuf("slot_i", [P, TOPK, NT], I32)
        lane_i = sbuf("lane_i", [P, TOPK, NT], I32)
        tile_i = sbuf("tile_i", [P, TOPK, NT], I32)
        tile_f = sbuf("tile_f", [P, TOPK, NT], F32)
        count_i = sbuf("count_i", [P, 2, E], I32)
        ends = sbuf("ends", [P, 2, 2 * E], F32)
        by_expert = sbuf("by_expert", [P, 2, E], F32)
        starts, tile_le = by_expert[:, 0], by_expert[:, 1]
        pack_sb = sbuf("pack_sb", [P, WORDS], F32)
        expert_words = sbuf("expert_words", [1, WORDS], I32)
        gather_at = sbuf("gather_at", [P, SLOT_TILES + 1], U32)
        softmax_row = sbuf("softmax_row", [P, 3, 2, 1], F32)
        row_max, row_sum, row_inv = (softmax_row[:, i] for i in range(3))
        bank = [ctx.enter_context(nc.psum_tensor(f"bank{i}", [P, BANK], F32)) for i in range(8)]

        s_const = counter("s_const")
        s_small = counter("s_small")
        s_fcb = counter("s_fcb")
        s_x = [counter(f"s_x{b}") for b in range(B)]
        s_stage = [counter(f"s_stage{i}") for i in range(4)]
        s_wsplit_hi = counter("s_wsplit_hi")
        s_wsplit_lo = counter("s_wsplit_lo")
        s_wsplit_lo_dve = counter("s_wsplit_lo_dve")
        s_raw = counter("s_raw")
        s_fold = counter("s_fold")
        s_fold_hi = counter("s_fold_hi")
        s_fold_lo = counter("s_fold_lo")
        s_ln = counter("s_ln")
        s_rstd = counter("s_rstd")
        s_xn_out = [counter(f"s_xn_out{i}") for i in range(XN_BUFS + 2)]
        s_t = counter("s_t")
        s_t_hi = counter("s_t_hi")
        s_t_lo = counter("s_t_lo")
        s_router = counter("s_router")
        s_score = counter("s_score")
        s_route = counter("s_route")
        s_rank = counter("s_rank")
        s_pick = counter("s_pick")
        s_pick_pool = counter("s_pick_pool")
        s_inv = counter("s_inv")
        s_row = [counter(f"s_row{i}") for i in range(4)]
        s_xrow = [counter(f"s_xrow{i}") for i in range(4)]
        s_gu = counter("s_gu")
        s_silu = counter("s_silu")
        s_act = counter("s_act")
        s_hT = counter("s_hT")
        s_hT_hi = counter("s_hT_hi")
        s_hT_lo = counter("s_hT_lo")
        s_y = counter("s_y")
        s_y_act = counter("s_y_act")
        s_y_out = [counter(f"s_y_out{i}") for i in range(3)]
        s_pair = [counter(f"s_pair{i}") for i in range(PAIRS)]
        s_res = counter("s_res")
        s_g = counter("s_g")
        s_g_hi = counter("s_g_hi")
        s_g_lo = counter("s_g_lo")
        s_s = counter("s_s")
        s_max = counter("s_max")
        s_exp = counter("s_exp")
        s_e_hi = counter("s_e_hi")
        s_e_lo = counter("s_e_lo")
        s_v = counter("s_v")
        s_inv_sum = counter("s_inv_sum")
        s_v_hi = counter("s_v_hi")
        s_v_lo = counter("s_v_lo")
        s_o = counter("s_o")
        s_out = counter("s_out")

        def three_pass(dst, lhs, rhs, first=True, last=True):
            n = len(lhs)
            for k in range(n):
                for i, (l, r) in enumerate(((0, 0), (0, 1), (1, 0))):
                    m = pe.matmul(dst, lhs[k][l], rhs[k][r], start=(first and k == 0 and i == 0),
                                  stop=(last and k == n - 1 and i == 2), skip_group_check=True)
            return m

        pool.memset(ident[:], 0.0)
        pool.memset(before[:], 1.0)
        pool.memset(minus_half, -0.5)
        pool.iota(expert_no[:], [[1, E]], base=0, channel_multiplier=0, allow_small_or_imprecise_dtypes=True)
        pool.iota(lane_no[:], [[1, P]], base=0, channel_multiplier=0, allow_small_or_imprecise_dtypes=True)
        pool.iota(tile_start, [[0, 1]], base=0, channel_multiplier=P, allow_small_or_imprecise_dtypes=True)
        pool.memset(ends[:], 0.0)
        pool.iota(tile_no16[:], [[1, SLOT_TILES + 1]], base=0, channel_multiplier=0,
                  allow_small_or_imprecise_dtypes=True)
        pool.iota(token_no[:], [[P, NT]], base=0, channel_multiplier=1, allow_small_or_imprecise_dtypes=True)
        zeroed = s_const.mark(pool.memset(ones[:], 1.0))
        wait(pool, zeroed)
        pool.affine_select(out=ident[:], in_=ident[:], compare_op=ALU.not_equal, fill=1.0, base=0,
                           pattern=[[-1, P]], channel_multiplier=1)
        constants = s_const.mark(pool.affine_select(out=before[:], in_=before[:], compare_op=ALU.is_gt, fill=0.0,
                                                    base=0, pattern=[[1, P]], channel_multiplier=-1))

        x_loaded = []
        for b in range(B):
            x_loaded.append(s_x[b].mark(sp.dma_start(
                x_sb[:, b * TB:(b + 1) * TB, :], x_rows[b * TB:(b + 1) * TB].rearrange("t p h -> p t h")), 16))
            if b == 0:
                act.dma_start(gate_raw[:], gate.rearrange("(k p) e -> p k e", p=P)).then_inc(s_small.handle, 16)
                act.dma_start(bias_sb[:], bias).then_inc(s_small.handle, 16)
                act.dma_start(pack_sb[:], pack).then_inc(s_small.handle, 16)
                s_small.value += 48
        small_loaded = (s_small, s_small.value)

        weight_ready = [None] * NW

        stages = [buf[:, i * WCOLS:(i + 1) * WCOLS] for buf in (stage, raw) for i in range(2)]
        split_done = [[] for _ in stages]

        def split_weight(n, w):
            i = n % len(stages)
            loaded = weight_loaded[n]
            cols = slice(w * WCOLS, (w + 1) * WCOLS)
            wait(act, loaded)
            hi = s_wsplit_hi.mark(act.copy(w_hi[:, cols], stages[i]))
            engine, sem = (dve, s_wsplit_lo_dve) if n % 3 == 2 else (pool, s_wsplit_lo)
            wait(engine, loaded, hi)
            lo = sem.mark(engine.tensor_tensor(w_lo[:, cols], stages[i], w_hi[:, cols].bitcast(F32), ALU.subtract))
            split_done[i] = [lo]
            weight_ready[w] = [lo]
            if n + len(stages) < NW:
                load_weight(n + len(stages))

        order = [E] + list(range(E))
        weight_loaded = {}

        def load_weight(n):
            i = n % len(stages)
            wait(sp, *split_done[i])
            weight_loaded[n] = s_stage[i].mark(sp.dma_start(stages[i], w_pack[order[n]]), 16)

        for n in range(len(stages)):
            load_weight(n)

        fold_in_free = []
        fold_in = route[:, 0:4, :].rearrange("p (m k) h -> p m k h", m=2)

        folds = [(is_v, head) for is_v in (False, True) for head in range(HEADS)]
        fold_loaded = []

        def load_fold():
            is_v, head = folds[len(fold_loaded)]
            left, right = (wv[head], fc_t) if is_v else (wq[head], wk[head])
            wait(sp, *fold_in_free)
            sp.dma_start(fold_in[:, 0], left.rearrange("(k p) h -> p k h", p=P)).then_inc(s_raw.handle, 16)
            s_raw.value += 16
            fold_loaded.append(s_raw.mark(sp.dma_start(fold_in[:, 1], right.rearrange("(k p) h -> p k h", p=P)), 16))

        FOLD_BANK = 6
        fold_bank_free, fold_made, folded = [], [], {}

        def fold():
            if len(fold_made) == len(folds):
                return
            wait(pe, fold_loaded[-1], *fold_bank_free)
            for e in range(KH):
                for k in range(KH):
                    m = pe.matmul(bank[FOLD_BANK][:, e * H:(e + 1) * H], fold_in[:, 0, k, e * P:(e + 1) * P],
                                  fold_in[:, 1, k, :], start=(k == 0), stop=(k == KH - 1))
            made = s_fold.mark(m)
            fold_made.append(made)
            fold_in_free[:] = [made]
            if len(fold_loaded) < len(folds):
                load_fold()

        def fold_split():
            if len(folded) == len(fold_made):
                return
            is_v, head = folds[len(folded)]
            dst, scale = (b_sp, 1.0 / HEADS) if is_v else (a_sp, Q_SCALE)
            src = bank[FOLD_BANK][:, 0:KH * H].rearrange("p (k h) -> p k h", k=KH)
            wait(act, fold_made[-1])
            hi = s_fold_hi.mark(act.mul(dst[:, 0, head], src, scale))
            wait(dve, hi)
            lo = s_fold_lo.mark(dve.scalar_tensor_tensor(out=dst[:, 1, head], in0=src, scalar=scale,
                                                         in1=dst[:, 0, head].bitcast(F32),
                                                         op0=ALU.mult, op1=ALU.subtract))
            fold_bank_free[:] = [lo]
            folded[(is_v, head)] = [lo]

        def norm_stats(t, ready):
            wait(dve, ready)
            return s_ln.mark(dve.bn_stats(stats[:, t // TB % 3, t % TB, :], x_sb[:, t, :]))

        def norm_scale(b, measured):
            for t in range(b * TB, (b + 1) * TB):
                wait(dve, measured[t])
                tok = s_ln.mark(dve.bn_aggr(moments[:, t, :], stats[:, t // TB % 3, t % TB, :]))
            cols = slice(b * TB, (b + 1) * TB)
            wait(dve, tok)
            tok = s_ln.mark(dve.tensor_scalar(variance[:, cols], moments[:, cols, 1], EPS, None, ALU.add))
            wait(pool, tok, constants)
            return s_rstd.mark(pool.tensor_tensor(rstd[:, cols], variance[:, cols], minus_half, ALU.pow))

        xn_bufs = [xn[:, i] for i in range(2)] + [raw[:, at:at + H] for at in (2 * WCOLS, 2 * WCOLS + H)]
        xn_ring = {"at": 0, "size": XN_BUFS}
        xn_free = [[] for _ in xn_bufs]

        def norm_rows(t, scaled):
            i = xn_ring["at"] % xn_ring["size"]
            xn_ring["at"] += 1
            wait(dve, scaled, *xn_free[i])
            xn_free[i] = []
            return i, s_ln.mark(dve.tensor_scalar(xn_bufs[i], x_sb[:, t, :], moments[:, t, 0:1], rstd[:, t:t + 1],
                                                  ALU.subtract, ALU.mult))

        gathers_done = []

        def store_rows(t, i, ready):
            wait(sp, ready, *gathers_done)
            stored = s_xn_out[i].mark(sp.dma_start(xn_dram[t * P:(t + 1) * P, :], xn_bufs[i]), 16)
            xn_free[i].append(stored)
            return stored

        class Ring:

            def __init__(self, places, free):
                self.places, self.free, self.at = places, [list(free) for _ in places], 0

            def users(self):
                return [tok for free in self.free for tok in free]

        def turn(src, ready, ring):
            j = ring.at % len(ring.places)
            ring.at += 1
            n, at = ring.places[j]
            ps = bank[n][:, at:at + KH * P].rearrange("p (k n) -> p k n", k=KH)
            wait(pe, constants, ready, *ring.free[j])
            for k in range(KH):
                m = pe.transpose(ps[:, k, :], src[:, k * P:(k + 1) * P], ident[:])
            return j, ps, s_t.mark(m)

        def split_turned(ring, j, ps, turned, hi_dst, lo_dst, dst_free):
            wait(act, turned, *dst_free)
            hi = s_t_hi.mark(act.copy(hi_dst, ps))
            wait(dve, hi, *dst_free)
            lo = s_t_lo.mark(dve.tensor_tensor(lo_dst, ps, hi_dst.bitcast(F32), ALU.subtract))
            ring.free[j] = [lo]
            return [lo]

        logits_all = bank[7][:, BANK - NT * E:]
        xt32 = [route[:, 4 + i, :].rearrange("p (k n) -> p k n", k=KH) for i in range(2)]
        xt32_free, xt32_full = [[], []], [None, None]

        def router_turn(t, ring, src, ready):
            i = t % 2
            j, ps, turned = turn(src, ready, ring)
            wait(act, turned, *xt32_free[i])
            xt32_full[i] = s_t_hi.mark(act.copy(xt32[i], ps))
            ring.free[j] = [xt32_full[i]]
            return turned

        side_ring = Ring(((7, 0),), [])

        def router(t, before):
            i = t % 2
            wait(pe, xt32_full[i], small_loaded, *side_ring.users(), *before)
            for k in range(KH):
                m = pe.matmul(logits_all[:, t * E:(t + 1) * E], xt32[i][:, k, :], gate_raw[:, k, :],
                              start=(k == 0), stop=(k == KH - 1), skip_group_check=True)
            logit[t] = s_router.mark(m)
            xt32_free[i] = [logit[t]]

        def tiles_by_expert(i, n=1):
            v = route[:, i:i + n, :].rearrange("p n (t e) -> p n t e", t=NT)
            return v[:, 0] if n == 1 else v

        score, biased, where = tiles_by_expert(0), tiles_by_expert(1), tiles_by_expert(6)
        picks, work = tiles_by_expert(2, TOPK), tiles_by_expert(4, TOPK)
        rank = bank[6][:, 0:(NT + 1) * E].rearrange("p (t e) -> p t e", t=NT + 1)
        index = bank[6][:, (NT + 1) * E:(NT + 1) * E + SLOT_TILES + 1]
        PICKERS = [(dve, s_pick), (pool, s_pick_pool), (dve, s_pick), (dve, s_pick)]
        PACKED_AT = (NT + 1) * E + SLOT_TILES + 1
        shift = P.bit_length() - 1

        def step(instruction):
            tok = s_route.mark(instruction)
            wait(dve, tok)
            return tok

        def choose(t0, t1, logits_ready, before):
            n = t1 - t0
            logits = logits_all[:, t0 * E:t1 * E].rearrange("p (t e) -> p t e", t=n)
            wait(act, logits_ready, *before)
            scored = s_score.mark(act.activation(score[:, t0:t1], logits, ACT.Sigmoid))
            side_ring.free[0] = side_ring.free[0] + [scored]
            yield
            wait(dve, scored, small_loaded, constants)
            step(dve.tensor_tensor(biased[:, t0:t1], score[:, t0:t1],
                                   bias_sb[:].unsqueeze(1).to_broadcast([P, n, E]), ALU.add))
            yield
            for t in range(t0, t1):
                tok = s_route.mark(dve.max(top8[:, t, :], biased[:, t, :]))
                if t % 4 == 3:
                    yield
            wait(dve, tok)
            for t in range(t0, t1):
                tok = s_route.mark(dve.max_index(top8_at[:, t, :], top8[:, t, :], biased[:, t, :]))
                if t % 4 == 3:
                    yield
            wait(dve, tok)
            step(dve.tensor_copy(top_at[:, :, t0:t1], top8_at[:, t0:t1, 0:TOPK].rearrange("p t k -> p k t")))
            for k in range(TOPK):
                tok = s_route.mark(dve.tensor_tensor(
                    picks[:, k, t0:t1], expert_no[:].unsqueeze(1).to_broadcast([P, n, E]),
                    top_at[:, k, t0:t1].unsqueeze(2).to_broadcast([P, n, E]), ALU.is_equal))
            yield
            wait(dve, tok)
            yield s_route.mark(dve.tensor_tensor(choice[:, t0:t1], picks[:, 0, t0:t1], picks[:, 1, t0:t1],
                                                         ALU.add))

        def assign(chosen, before_rank, routed):
            wait(pe, constants, *chosen, *before_rank)
            for t in range(NT):
                pe.matmul(rank[:, t, :], before[:], choice[:, t, :], start=(t == 0), stop=False,
                          skip_group_check=True)
                m = pe.matmul(rank[:, t + 1:NT + 1, :], ones[:],
                              choice[:, t, :].unsqueeze(1).to_broadcast([P, NT - t, E]), start=False,
                              stop=(t == NT - 1), skip_group_check=True)
            ranked = s_rank.mark(m)
            yield
            wait(dve, ranked)
            step(dve.tensor_scalar(count_i[:, 0, :], rank[:, NT, :], float(P - 1), None, ALU.add))
            step(dve.tensor_scalar(count_i[:, 1, :], count_i[:, 0, :], shift, shift,
                                   ALU.logical_shift_right, ALU.logical_shift_left))
            step(dve.tensor_copy(ends[:, 0, E:], count_i[:, 1, :]))
            d, i = 1, 0
            while d < E:
                step(dve.tensor_tensor(ends[:, 1 - i, E:], ends[:, i, E:], ends[:, i, E - d:2 * E - d], ALU.add))
                d, i = d * 2, 1 - i
            end = ends[:, i, E:]
            step(dve.tensor_tensor(starts, end, count_i[:, 1, :], ALU.subtract))
            yield
            step(dve.tensor_tensor(where, rank[:, 0:NT, :], starts.unsqueeze(1).to_broadcast([P, NT, E]), ALU.add))
            step(dve.tensor_tensor(work, picks, where.unsqueeze(1).to_broadcast([P, TOPK, NT, E]), ALU.mult))
            yield
            step(dve.tensor_reduce(slot[:], work, AX, ALU.add))
            routed["slots"] = step(dve.tensor_copy(slot_i[:], slot[:]))
            tok = s_route.mark(dve.tensor_scalar(lane_i[:], slot_i[:], P - 1, None, ALU.bitwise_and))
            step(dve.tensor_scalar(tile_i[:], slot_i[:], shift, None, ALU.logical_shift_right))
            split = step(dve.tensor_copy(tile_f[:], tile_i[:]))
            yield
            step(dve.tensor_scalar(tile_le, end, tile_start, None, ALU.is_le))
            step(dve.tensor_reduce(tile_expert, tile_le, AX, ALU.add))
            numbered = step(dve.tensor_scalar(tile_expert, tile_expert, float(E - 1), None, ALU.min))
            wait(pe, numbered, small_loaded)
            packed = s_rank.mark(pe.matmul(bank[6][0:1, PACKED_AT:PACKED_AT + WORDS], tile_expert, pack_sb[:],
                                           start=True, stop=True, skip_group_check=True))
            wait(dve, packed)
            routed["experts"] = step(dve.tensor_copy(expert_words[:], bank[6][0:1, PACKED_AT:PACKED_AT + WORDS]))
            pairs_of = [(t, k) for t in range(NT) for k in range(TOPK)]
            used, made = [None] * PICKS, [None] * PICKS
            GROUP = PICKS // 2
            for n0 in range(0, len(pairs_of) + GROUP, GROUP):
                for n in range(max(n0 - GROUP, 0), n0):
                    i = n % PICKS
                    wait(pe, made[i])
                    used[i] = s_inv.mark(pe.matmul(index, pick_lane[:, i, :], pick_tile[:, i, :],
                                                   start=(n == 0), stop=(n == len(pairs_of) - 1)))
                for n in range(n0, min(n0 + GROUP, len(pairs_of))):
                    (t, k), i = pairs_of[n], n % PICKS
                    engine, sem = PICKERS[i]
                    wait(engine, used[i], split)
                    sem.mark(engine.tensor_scalar(pick_lane[:, i, :], lane_no[:], lane_i[:, k, t:t + 1], None,
                                                  ALU.is_equal))
                    made[i] = sem.mark(engine.tensor_scalar(pick_tile[:, i, :], tile_no16[:], tile_f[:, k, t:t + 1],
                                                            token_no[:, t:t + 1], ALU.is_equal, ALU.mult))
                yield
            wait(dve, used[n % PICKS])
            routed["indexed"] = s_route.mark(dve.tensor_copy(gather_at[:], index))

        def gate_weights(routed):
            step(dve.tensor_tensor(work, picks, score.unsqueeze(1).to_broadcast([P, TOPK, NT, E]), ALU.mult))
            yield
            step(dve.tensor_reduce(weight[:], work, AX, ALU.add))
            step(dve.tensor_tensor(total_w[:], weight[:, 0, :], weight[:, 1, :], ALU.add))
            step(dve.tensor_scalar(total_w[:], total_w[:], 1e-20, None, ALU.add))
            step(dve.reciprocal(total_w[:], total_w[:]))
            for k in range(TOPK):
                routed["weights"] = s_route.mark(dve.scalar_tensor_tensor(
                    out=weight[:, k, :], in0=weight[:, k, :], scalar=0.5, in1=total_w[:], op0=ALU.mult, op1=ALU.mult))
            yield

        row_buf = raw[:, 0:1024].rearrange("p (i h) -> p i h", i=4)
        y_buf = raw[:, 1024:1792].rearrange("p (i h) -> p i h", i=3)
        h_buf = raw[:, 1792:2048].rearrange("p (i f) -> p i f", i=2)
        ht_rows = e_sp[:].rearrange("p a s n -> p (a s n)")[:, 0:4 * P].rearrange("p (i s n) -> p i s n", s=2, n=P)
        SHARED, SLOT = "shared", "slot"
        H_LAG, LAG = 3, 4

        def ffn(routed, early, xt_half, ring, before, raw_before, between):
            xt_ring = xT[:, xt_half].rearrange("p s k n -> p (s k n)").rearrange("p (i s k n) -> p i s k n", s=2,
                                                                                 k=KH, n=P)
            row_free = [list(raw_before) for _ in range(4)]
            xt_free, xt_ready = [list(before) for _ in range(3)], [None] * 3
            h_free, h_ready, hT_bank_free = [list(raw_before), list(raw_before)], [None, None], list(before)
            ht_free, gu_free, y_free = [list(before), list(before)], [list(before), list(before)], list(before)
            items = ([(SHARED, t) for t in range(early)] + [(SLOT, j) for j in range(SLOT_TILES)]
                     + [(SHARED, t) for t in range(early, NT)])
            ht_ready = [None, None]
            weights, word = {}, {}
            last_row = {}

            def load(n):
                kind, j = items[n]
                i = n % 4
                if kind == SHARED:
                    wait(sp, stored[j], *row_free[i])
                    return s_xrow[i].mark(sp.dma_start(row_buf[:, i, :], xn_dram[j * P:(j + 1) * P, :]), 16)
                wait(pool, *stored, routed["indexed"], *row_free[i])
                last_row[i] = s_row[i].mark(pool.indirect_dma_start(
                    row_buf[:, i, :], None, xn_dram, bass.IndirectOffsetOnAxis(ap=gather_at[:, j:j + 1], axis=0)), 16)
                return last_row[i]

            loads = []

            def load_ahead(s):
                while len(loads) < min(s + 4, len(items)):
                    kind, j = items[len(loads)]
                    if len(loads) > s and (stored[j] is None if kind == SHARED else "indexed" not in routed):
                        break
                    loads.append(load(len(loads)))

            def pick_weights(n):
                kind, j = items[n]
                if kind == SHARED:
                    return lambda part, at, size: (w_hi, w_lo)[part][:, E * WCOLS + at:E * WCOLS + at + size]
                wait(pe, routed["experts"])
                if j % PER_LOAD == 0:
                    word["value"] = pe.value_load(expert_words[0:1, j // PER_LOAD:j // PER_LOAD + 1], min_val=0,
                                                  max_val=E ** PER_LOAD - 1)
                base = ((word["value"] >> (E_BITS * (j % PER_LOAD))) & (E - 1)) * WCOLS
                return lambda part, at, size: (w_hi, w_lo)[part][:, bass.ds(base + at, size)]

            def sink(n, y, made):
                kind, j = items[n]
                if kind == SHARED:
                    wait(dve, made, residual[j])
                    residual[j] = s_res.mark(dve.scalar_tensor_tensor(
                        out=x_sb[:, j, :], in0=y, scalar=0.5, in1=x_sb[:, j, :], op0=ALU.mult, op1=ALU.add))
                    return residual[j]
                i = j % 3
                wait(act, made, *y_stores[i], *(raw_before if j < 3 else []))
                copied = s_y_act.mark(act.copy(y_buf[:, i, :], y))
                wait(sp, copied, *pairs_read)
                y_stores[i] = [s_y_out[i].mark(sp.dma_start(y_dram[j * P:(j + 1) * P, :], y_buf[:, i, :]), 16)]
                return copied

            for s in range(len(items) + LAG):
                d, g, v = s - LAG, s - 1, s - H_LAG
                load_ahead(s)
                if 0 <= v < len(items):
                    c = v % 2
                    wait(pe, h_ready[c], *hT_bank_free)
                    turned = s_hT.mark(pe.transpose(bank[4][:, 0:P], h_buf[:, c, :], ident[:]))
                    h_free[c] = [turned]
                    wait(act, turned, *ht_free[c])
                    hi = s_hT_hi.mark(act.copy(ht_rows[:, c, 0], bank[4][:, 0:P]))
                    wait(dve, hi)
                    lo = s_hT_lo.mark(dve.tensor_tensor(ht_rows[:, c, 1], bank[4][:, 0:P],
                                                        ht_rows[:, c, 0].bitcast(F32), ALU.subtract))
                    hT_bank_free = ht_ready[c] = [lo]
                if s < len(items):
                    j, ps, turned = turn(row_buf[:, s % 4, :], loads[s], ring)
                    row_free[s % 4] = [turned]
                    xt_ready[s % 3] = split_turned(ring, j, ps, turned, xt_ring[:, s % 3, 0], xt_ring[:, s % 3, 1],
                                                   xt_free[s % 3])
                if 0 <= g < len(items):
                    c = g % 2
                    if g == 0:
                        weights[0] = pick_weights(0)
                        wait(pe, *weight_ready[E])
                    if g == early:
                        for w in range(NW):
                            wait(pe, *weight_ready[w])
                    wait(pe, *xt_ready[g % 3], *gu_free[c])
                    gu = bank[2 + c][:, 0:GU]
                    lhs = [[xt_ring[:, g % 3, part, k, :] for part in range(2)] for k in range(KH)]
                    rhs = [[weights[g](part, k * GU, GU) for part in range(2)] for k in range(KH)]
                    made = s_gu.mark(three_pass(gu, lhs, rhs))
                    xt_free[g % 3] = [made]
                    wait(act, made, *h_free[c])
                    silu = s_silu.mark(act.activation(h_buf[:, c, :], gu[:, 0:F], ACT.Silu))
                    wait(dve, silu)
                    h_ready[c] = s_act.mark(dve.tensor_tensor(h_buf[:, c, :], h_buf[:, c, :], gu[:, F:GU], ALU.mult))
                    gu_free[c] = [h_ready[c]]
                    if g + 1 < len(items):
                        weights[g + 1] = pick_weights(g + 1)
                if d >= 0:
                    c = d % 2
                    w = weights.pop(d)
                    wait(pe, *ht_ready[c], *y_free)
                    y = bank[5][:, 0:H]
                    made = s_y.mark(three_pass(y, [[ht_rows[:, c, 0], ht_rows[:, c, 1]]],
                                               [[w(0, KH * GU, H), w(1, KH * GU, H)]]))
                    ht_free[c] = [made]
                    y_free = [sink(d, y, made)]
                between(s, s >= early + SLOT_TILES - 1 + LAG)
            gathers_done[:] = list(last_row.values())
            return [*y_free, *hT_bank_free, *gu_free[0], *gu_free[1], *ht_free[0], *ht_free[1], *ring.users(),
                    *xt_free[0], *xt_free[1], *xt_free[2], *h_free[0], *h_free[1], *row_free[0], *row_free[1],
                    *row_free[2], *row_free[3]]

        y_stores = [[], [], []]
        pairs_read = []
        pair_buf = stage[:].rearrange("p (i h) -> p i h", i=PAIRS)
        pair_free = [[] for _ in range(PAIRS)]

        def gather_pair(t, routed):
            toks = []
            for k in range(TOPK):
                i = (t * TOPK + k) % PAIRS
                wait(pool, routed["slots"], *[s for ss in y_stores for s in ss], *pair_free[i],
                     *[tok for done in split_done for tok in done])
                toks.append(s_pair[i].mark(pool.indirect_dma_start(
                    pair_buf[:, i, :], None, y_dram,
                    bass.IndirectOffsetOnAxis(ap=slot_i[:, k, t:t + 1].bitcast(U32), axis=0)), 16))
            pairs_read.extend(toks)
            del pairs_read[:-PAIRS]
            return toks

        def combine(t, toks, routed, ready):
            for k in range(TOPK):
                i = (t * TOPK + k) % PAIRS
                wait(dve, toks[k], ready, routed["weights"])
                ready = s_res.mark(dve.scalar_tensor_tensor(
                    out=x_sb[:, t, :], in0=pair_buf[:, i, :], scalar=weight[:, k, t:t + 1], in1=x_sb[:, t, :],
                    op0=ALU.mult, op1=ALU.add))
                pair_free[i] = [ready]
            return ready

        def run(generator):
            for _ in generator:
                pass

        residual = [x_loaded[t // TB] for t in range(NT)]
        stored, logit = [None] * NT, [None] * NT
        measured, scaled = [None] * NT, [None] * B
        splits = iter(enumerate(order))

        def next_split():
            for n, w in splits:
                split_weight(n, w)
                break

        def measure(b):
            for t in range(b * TB, (b + 1) * TB):
                measured[t] = norm_stats(t, residual[t])
            scaled[b] = norm_scale(b, measured)

        def ffn_front(b, ring, before):
            rows = {}
            for q in range(TB + 2):
                if q >= 2 and ring is side_ring:
                    router(b * TB + q - 2, before)
                if 1 <= q <= TB:
                    i, done = rows.pop(q - 1)
                    xn_free[i].append(router_turn(b * TB + q - 1, ring, xn_bufs[i], done))
                if q >= 2 and ring is not side_ring:
                    router(b * TB + q - 2, before)
                if q < TB:
                    rows[q] = norm_rows(b * TB + q, scaled[b])
                    stored[b * TB + q] = store_rows(b * TB + q, *rows[q])
                yield

        def routing(routed, picked, before_rank):
            yield from assign(picked, before_rank, routed)
            yield from gate_weights(routed)

        def choose_into(picked, b0, b1, before):
            for got in choose(b0 * TB, b1 * TB, logit[b1 * TB - 1], before):
                yield
            picked.append(got)

        routed1, picked1, pairs = {}, [], {}

        front_ring = Ring(((6, 0),), [])

        def front1():
            measure(0)
            yield
            for b in range(B):
                if b + 1 < B:
                    measure(b + 1)
                    yield
                yield from ffn_front(b, front_ring, [])
            yield from choose_into(picked1, 0, B, [])
            yield from routing(routed1, picked1, front_ring.users())

        attn_in = [None] * NT
        xt_batch_free = [[], []]
        fcb = {}

        def attn_front(b):
            AHEAD = 2
            for q in range(TB + AHEAD):
                if q >= AHEAD:
                    t = b * TB + q - AHEAD
                    residual[t] = combine(t, pairs[t], routed1, residual[t])
                    measured[t] = norm_stats(t, residual[t])
                if q < TB:
                    pairs[b * TB + q] = gather_pair(b * TB + q, routed1)
                if q == TB + AHEAD - 1:
                    scaled[b] = norm_scale(b, measured)
                yield
            rows = {}
            for q in range(TB + 1):
                t = b * TB + q
                if q > 0:
                    i, done = rows.pop(q - 1)
                    cols = slice((q - 1) * P, q * P)
                    j, ps, turned = turn(xn_bufs[i], done, side_ring)
                    attn_in[t - 1] = split_turned(side_ring, j, ps, turned, xT[:, b % 2, 0, :, cols],
                                                  xT[:, b % 2, 1, :, cols], xt_batch_free[b % 2])
                    xn_free[i].append(turned)
                if q < TB:
                    rows[q] = norm_rows(t, scaled[b])
                    wait(dve, rows[q][1], fcb["loaded"])
                    residual[t] = s_res.mark(dve.tensor_tensor(x_sb[:, t, :], x_sb[:, t, :], fcb_sb, ALU.add))
                yield

        r1, a0 = front1(), attn_front(0)
        PIECES_AHEAD = 50
        EARLY1, PIECES1 = 8, 3
        FOLD_EVERY = 24
        next(r1)
        next(r1)
        for n in range(PIECES_AHEAD):
            if NW * (n + 1) // PIECES_AHEAD > NW * n // PIECES_AHEAD:
                next_split()
            next(r1)

        def between1(s, gathering):
            if s < EARLY1:
                for _ in range(PIECES1):
                    next(r1, None)
                if s == EARLY1 - 1:
                    run(r1)
                    fold_in_free[:] = [routed1["weights"]]
                    load_fold()
                    wait(sp, routed1["slots"])
                    fcb["loaded"] = s_fcb.mark(sp.dma_start(fcb_sb, fc_b), 16)
            elif s % (2 if gathering else FOLD_EVERY) == 1:
                fold()
            else:
                fold_split()
            if gathering:
                next(a0, None)

        ring = Ring(((0, 0), (1, 0)), [])
        xn_ring["size"] = 2
        raw_users = [tok for toks in split_done[2:] + xn_free[2:] for tok in toks]
        ffn1_users = ffn(routed1, EARLY1, 1, ring, [], raw_users, between1)
        while len(folded) < len(folds):
            fold_split()
            fold()
        run(a0)

        e32 = raw[:, 0:2 * N].rearrange("p (i n) -> p i n", i=2)
        S_BANKS, G_BANKS, V_BANK, O_BANKS = (0, 1), (2, 6), 3, (4, 5)
        y1_stored = [tok for toks in y_stores for tok in toks]
        g_bank_free, g_free = [list(ffn1_users), list(ffn1_users)], []
        s_free = [list(ffn1_users), list(ffn1_users)]
        v_bank_free, o_free = list(ffn1_users), list(ffn1_users)
        e_free, v_free = [list(ffn1_users), list(ffn1_users)], [[], []]
        e32_free = [ffn1_users + y1_stored, ffn1_users + y1_stored]
        xn_ring["size"] = XN_BUFS
        xn_free[2:] = [ffn1_users + y1_stored, ffn1_users + y1_stored]
        g_made, g_ready = [None, None], [None, None]
        units = [(b, h, m) for b in range(B) for h in range(HEADS) for m in range(TB)]
        scores_done, pv_ready = {}, {}

        def make_g(b, h, f):
            wait(pe, *[tok for t in range(b * TB, (b + 1) * TB) for tok in attn_in[t]], *folded[(False, h)],
                 *g_bank_free[f])
            lhs = [[a_sp[:, part, h, k, f * P:(f + 1) * P] for part in range(2)] for k in range(KH)]
            rhs = [[xT[:, b % 2, part, k, :] for part in range(2)] for k in range(KH)]
            g_made[f] = s_g.mark(three_pass(bank[G_BANKS[f]][:], lhs, rhs))

        def split_g_hi(f):
            wait(act, g_made[f], *g_free)
            g_ready[f] = [s_g_hi.mark(act.copy(g_sp[:, 0, f, :], bank[G_BANKS[f]][:]))]

        def split_g_lo(f):
            wait(dve, *g_ready[f])
            g_ready[f] = [s_g_lo.mark(dve.tensor_tensor(g_sp[:, 1, f, :], bank[G_BANKS[f]][:],
                                                         g_sp[:, 0, f, :].bitcast(F32), ALU.subtract))]
            g_bank_free[f] = g_ready[f]

        def attn_scores(u):
            b, h, m = units[u]
            i = u % 2
            keys = slice(m * P, (m + 1) * P)
            wait(pe, *g_ready[0], *g_ready[1], *s_free[i])
            lhs = [[xT[:, b % 2, part, k, keys] for part in range(2)] for k in range(KH)]
            rhs = [[g_sp[:, part, k, :] for part in range(2)] for k in range(KH)]
            scores_done[u] = s_s.mark(three_pass(bank[S_BANKS[i]][:], lhs, rhs))

        def attn_max(u):
            i = u % 2
            wait(dve, scores_done[u])
            return s_max.mark(dve.tensor_reduce(row_max[:, i, :], bank[S_BANKS[i]][:], AX, ALU.max, negate=True))

        def attn_exp(u, mx):
            i = u % 2
            wait(act, mx, *e32_free[i])
            ex = s_exp.mark(act.activation(e32[:, i, :], bank[S_BANKS[i]][:], ACT.Exp, bias=row_max[:, i, :],
                                           accum_out=row_sum[:, i, :]))
            s_free[i] = [ex]
            return ex

        def attn_split(u, ex):
            i = u % 2
            wait(act, ex, *e_free[i])
            hi = s_e_hi.mark(act.copy(e_sp[:, i, 0, :], e32[:, i, :]))
            wait(dve, ex)
            iv = s_inv_sum.mark(dve.reciprocal(row_inv[:, i, :], row_sum[:, i, :]))
            wait(pool, hi, *e_free[i])
            lo = s_e_lo.mark(pool.tensor_tensor(e_sp[:, i, 1, :], e32[:, i, :], e_sp[:, i, 0, :].bitcast(F32),
                                                ALU.subtract))
            e32_free[i] = [lo]
            return iv, lo

        def attn_values(u, iv, e_lo):
            nonlocal v_bank_free
            b, h, m = units[u]
            i = u % 2
            keys = slice(m * P, (m + 1) * P)
            wait(pe, *v_bank_free, *folded[(True, h)])
            v_ps = bank[V_BANK][:, 0:H]
            lhs = [[xT[:, b % 2, part, k, keys] for part in range(2)] for k in range(KH)]
            rhs = [[b_sp[:, part, h, k, :] for part in range(2)] for k in range(KH)]
            made = s_v.mark(three_pass(v_ps, lhs, rhs))
            wait(act, made, iv, *v_free[i])
            hi = s_v_hi.mark(act.mul(v_sp[:, i, 0, :], v_ps, row_inv[:, i, :]))
            wait(dve, hi, *v_free[i])
            lo = s_v_lo.mark(dve.scalar_tensor_tensor(out=v_sp[:, i, 1, :], in0=v_ps, scalar=row_inv[:, i, :],
                                                      in1=v_sp[:, i, 0, :].bitcast(F32), op0=ALU.mult,
                                                      op1=ALU.subtract))
            v_bank_free = [lo]
            pv_ready[u] = [e_lo, lo]
            return made

        def mix(u):
            b, h, m = units[u]
            i = u % 2
            first, last = (h == 0 and m == 0), (h == HEADS - 1 and m == TB - 1)
            wait(pe, *pv_ready[u], *(o_free if first else []))
            for q in range(TB):
                dst = bank[O_BANKS[q // 2]][:, (q % 2) * H:(q % 2 + 1) * H]
                lhs = [[e_sp[:, i, part, q * P:(q + 1) * P] for part in range(2)]]
                rhs = [[v_sp[:, i, part, :] for part in range(2)]]
                mm = three_pass(dst, lhs, rhs, first=(first and q % 2 == 0), last=last)
            done = s_o.mark(mm)
            e_free[i], v_free[i] = [done], [done]
            if last:
                attn_out(b, done)
            return u + 1

        def attn_out(b, done):
            nonlocal o_free
            for q in range(TB):
                t = b * TB + q
                wait(dve, done, residual[t])
                residual[t] = s_res.mark(dve.tensor_tensor(
                    x_sb[:, t, :], x_sb[:, t, :], bank[O_BANKS[q // 2]][:, (q % 2) * H:(q % 2 + 1) * H], ALU.add))
            o_free = [residual[t]]

        routed2, picked2 = {}, []
        PER_BATCH = HEADS * TB
        U = len(units)

        def previous_front(b):
            yield
            yield
            measure(b - 1)
            yield
            yield from ffn_front(b - 1, side_ring, [])
            if b == B - 1:
                yield from choose_into(picked2, 0, b, [routed1["weights"]])

        for f in range(KH):
            make_g(0, 0, f)
            split_g_hi(f)
            split_g_lo(f)
        mixed = 0
        sides = []
        for u in range(U):
            b, h, m = units[u]
            if h == 0 and m == 0:
                sides = [attn_front(b + 1)] if b + 1 < B else []
                if b > 0:
                    sides.append(previous_front(b))
            nxt = units[u + 1] if (m == TB - 1 and u + 1 < U) else None
            if m == 0 and mixed < u - 1:
                mixed = mix(mixed)
            if nxt:
                for f in range(KH):
                    make_g(nxt[0], nxt[1], f)
            attn_scores(u)
            if nxt:
                g_free = [scores_done[u]]
                split_g_hi(0)
            mx = attn_max(u)
            if nxt:
                split_g_hi(1)
                split_g_lo(0)
                split_g_lo(1)
            ex = attn_exp(u, mx)
            if mixed < u - 1:
                mixed = mix(mixed)
            next(sides[0], None)
            iv, e_lo = attn_split(u, ex)
            vmade = attn_values(u, iv, e_lo)
            if u % PER_BATCH == PER_BATCH - 1:
                xt_batch_free[b % 2] = [vmade, scores_done[u]]
            if len(sides) > 1:
                next(sides[1], None)
            if b == B - 1 and u % PER_BATCH >= PER_BATCH // 2:
                next(sides[-1], None)
        while mixed < U:
            mixed = mix(mixed)

        attention_done = [*o_free, *xt_batch_free[0], *xt_batch_free[1], *s_free[0], *s_free[1], *v_bank_free,
                          *g_bank_free[0], *g_bank_free[1]]
        xn_raw_free = xn_free[2] + xn_free[3]
        xn_bufs[2:] = [pair_buf[:, i, :] for i in range(2)]
        xn_free[2:] = [list(pair_free[i]) for i in range(2)]
        s_xn_out[2:] = s_xn_out[4:]
        EARLY2, PIECES2 = 8, 6

        front_ring.free[0] = attention_done

        def front2():
            measure(B - 1)
            yield
            yield from ffn_front(B - 1, front_ring, attention_done)
            yield from sides[0]
            yield from choose_into(picked2, B - 1, B, [routed1["weights"]])
            yield from routing(routed2, picked2, front_ring.users())

        tail = {}

        def tail2():
            for i in range(2):
                pair_free[i] += xn_free[2 + i]
            AHEAD = 2
            for t in range(NT + AHEAD):
                if t < NT:
                    pairs[t] = gather_pair(t, routed2)
                if t >= AHEAD:
                    q = t - AHEAD
                    ready = combine(q, pairs[q], routed2, residual[q])
                    wait(sp, ready)
                    tail["stored"] = s_out.mark(sp.dma_start(out_rows[q], x_sb[:, q, :]), 16)
                yield

        r2, t2 = front2(), tail2()

        def between2(s, gathering):
            if s < EARLY2:
                for _ in range(PIECES2):
                    next(r2, None)
                if s == EARLY2 - 1:
                    run(r2)
            if gathering:
                next(t2, None)

        ring = Ring(((0, 0), (1, 0)), attention_done)
        ffn(routed2, EARLY2, 0, ring, attention_done, [*e32_free[0], *e32_free[1], *xn_raw_free], between2)
        run(t2)
        wait(sp, tail["stored"])


def kernel(L0_attn_x, L0_attn_Wq, L0_attn_Wk, L0_attn_Wv, L0_attn_fc_w, L0_attn_fc_b, L0_ffn_gate_w,
           L0_ffn_expert_bias, L0_ffn_shared_gate_w, L0_ffn_shared_up_w, L0_ffn_shared_down_w,
           L0_ffn_experts_gate_up, L0_ffn_experts_down):
    import concourse.bacc as bacc
    from concourse.bass_utils import run_bass_kernel_spmd

    shared_gu = np.concatenate([L0_ffn_shared_gate_w, L0_ffn_shared_up_w], axis=1)[None]
    gate_up = np.concatenate([L0_ffn_experts_gate_up, shared_gu])
    down = np.concatenate([L0_ffn_experts_down, np.asarray(L0_ffn_shared_down_w)[None]])
    nw, hidden, gu = gate_up.shape
    gate_up = gate_up.reshape(nw, hidden // P, P, gu).transpose(0, 2, 1, 3).reshape(nw, P, -1)
    arrays = {
        "x": L0_attn_x,
        "w_pack": np.concatenate([gate_up, down], axis=2),
        "wq": L0_attn_Wq,
        "wk": L0_attn_Wk,
        "wv": L0_attn_Wv,
        "fc_t": np.asarray(L0_attn_fc_w).T,
        "fc_b": np.broadcast_to(np.asarray(L0_attn_fc_b), (P, hidden)),
        "gate": L0_ffn_gate_w,
        "bias": np.broadcast_to(np.asarray(L0_ffn_expert_bias), (P, nw - 1)),
    }
    experts, per = nw - 1, tiles_per_word(nw - 1)
    tile = np.arange(P)[:, None]
    words = np.arange(-(-(L0_attn_x.shape[0] * L0_attn_x.shape[1] * 2 // P + experts - 1) // per))[None]
    arrays["pack"] = np.where(tile // per == words, float(experts) ** (tile % per), 0.0).astype(np.float32)
    arrays = {f"in_{k}": np.ascontiguousarray(v) for k, v in arrays.items()}
    nc = bacc.Bacc("TRN2", target_bir_lowering=False, num_devices=1)
    args = [nc.dram_tensor(k, v.shape, mybir.dt.from_np(v.dtype), kind="ExternalInput").ap() for k, v in arrays.items()]
    out = nc.dram_tensor("out", arrays["in_x"].shape, F32, kind="ExternalOutput").ap()
    macaron(nc, *args, out)
    result = run_bass_kernel_spmd(nc, [arrays], core_ids=[0])
    return result.results[0]["out"]
```
